# Optimizing a Trainium2 kernel written in Bass

```python
import numpy as np
import jax
import jax.numpy as jnp

def _softmax(x, axis=-1):
    return jax.nn.softmax(x, axis=axis)

def _gelu(x):
    return jax.nn.gelu(x, approximate=True)

def _silu(x):
    return jax.nn.silu(x)

def _sigmoid(x):
    return jax.nn.sigmoid(x)

def _layernorm(x, axis=-1, eps=1e-05):
    m = jnp.mean(x, axis=axis, keepdims=True)
    v = jnp.var(x, axis=axis, keepdims=True)
    return (x - m) / jnp.sqrt(v + eps)

def _scatter_add(tgt, idx, src, axis=0):
    return tgt.at[idx].add(src)

def _segment_sum(src, seg, n):
    return jax.ops.segment_sum(src, seg, n)
kernel_name = 'mk_flamingo_gated_d2_seqx_r8_d25e2c'

def setup_inputs(seed: int=0):
    np.random.seed(seed)
    _w = jnp.asarray

    def _rec_inputs():
        import jax
        import jax.numpy as jnp
        _rk = jax.random.key(seed)
        x = 0.0003765 + 1 * jax.random.normal(jax.random.fold_in(_rk, 1), (8, 128, 256), jnp.float32)
        _lenS = 128 - jax.random.randint(jax.random.fold_in(_rk, 7), (8,), 0, max(1, 128 // 4) + 1, jnp.int32)
        _lenS2 = 128 - jax.random.randint(jax.random.fold_in(_rk, 8), (8,), 0, max(1, 128 // 4) + 1, jnp.int32)
        _ctx_2048P = jax.random.normal(jax.random.fold_in(_rk, 11), (8, 16, 256), jnp.float32)
        _ctx_2048c = jax.random.dirichlet(jax.random.fold_in(_rk, 511), 0.3 * jnp.ones((16,), jnp.float32), (8, 128))
        _ctx_2048t = jnp.einsum('bsk,bkd->bsd', _ctx_2048c, _ctx_2048P)
        _ctx_2048t = _ctx_2048t * jax.lax.rsqrt(jnp.mean(jnp.square(_ctx_2048t)) + 1e-12) * 0.953939
        ctx_2048 = -0.000292821 + 1.00034 * (_ctx_2048t + 0.3 * jax.random.normal(jax.random.fold_in(_rk, 611), (8, 128, 256), jnp.float32))
        _g = jax.random.normal(jax.random.fold_in(_rk, 9001), (2, 2), jnp.float32)
        _g = jnp.sign(_g) * jnp.maximum(jnp.abs(_g), 1.0) + (_g == 0) * 1.0
        g_xattn = _g[0]
        g_ffn = _g[1]
        return (x, ctx_2048, g_xattn, g_ffn)
    x, ctx_2048, g_xattn, g_ffn = _rec_inputs()

    def _L0_xattn_setup():
        import jax, jax.numpy as jnp
        import numpy as np
        key = jax.random.key(seed)
        k1, k2, k3, k4, k5 = jax.random.split(key, 5)
        B, D_MODEL, L = (2, 128, 256)
        HEAD_DIM = 8
        H = D_MODEL // HEAD_DIM
        return {'k': jax.random.normal(k1, (B, D_MODEL, L), dtype=jnp.float32), 'v': jax.random.normal(k2, (B, D_MODEL, L), dtype=jnp.float32), 'q': jax.random.normal(k3, (B, D_MODEL, L), dtype=jnp.float32), 'ssm_kernel': jax.random.normal(k4, (H, L), dtype=jnp.float32), 'D': jax.random.normal(k5, (H,), dtype=jnp.float32), 'head_dim': HEAD_DIM}
    _L0_xattn_all = _L0_xattn_setup()
    _L0_xattn_in = {k: v for k, v in _L0_xattn_all.items() if k in ('ssm_kernel', 'D')}
    del _L0_xattn_all

    def _L0_ffn_setup():
        import jax, jax.numpy as jnp
        import numpy as np
        TOPK = 6
        CAP = 128
        ROUTE_SCALE = 1.0
        key = jax.random.key(seed)
        k = jax.random.split(key, 6)
        B, T, C = (2, 256, 256)
        E, H, HS = (64, 32, 64)
        std = 0.01
        return {'x': jax.random.normal(k[0], (B, T, C), jnp.float32), 'w_gate': jax.random.normal(k[1], (C, E), jnp.float32) * std, 'w_shared_up': jax.random.normal(k[2], (C, 2 * HS), jnp.float32) * std, 'w_shared_down': jax.random.normal(k[3], (HS, C), jnp.float32) * std, 'w_up': jax.random.normal(k[4], (E, C, 2 * H), jnp.float32) * std, 'w_down': jax.random.normal(k[5], (E, H, C), jnp.float32) * std}
    _L0_ffn_all = _L0_ffn_setup()
    _L0_ffn_in = {k: v for k, v in _L0_ffn_all.items() if k in ('w_gate', 'w_shared_up', 'w_shared_down', 'w_up', 'w_down')}
    del _L0_ffn_all

    def _L1_xattn_setup():
        import jax, jax.numpy as jnp
        import numpy as np

        def _wkv(time_decay, time_first, k, v):
            w = -jnp.exp(time_decay)
            u = time_first
            B, T, C = k.shape
            aa = jnp.zeros((B, C), dtype=k.dtype)
            bb = jnp.zeros((B, C), dtype=k.dtype)
            pp = jnp.full((B, C), -1e+38, dtype=k.dtype)

            def step(carry, kv_t):
                aa, bb, pp = carry
                kt, vt = kv_t
                ww = u + kt
                q = jnp.maximum(pp, ww)
                e1 = jnp.exp(pp - q)
                e2 = jnp.exp(ww - q)
                y_t = (e1 * aa + e2 * vt) / (e1 * bb + e2)
                ww2 = pp + w
                q2 = jnp.maximum(ww2, kt)
                e1b = jnp.exp(ww2 - q2)
                e2b = jnp.exp(kt - q2)
                new_carry = (e1b * aa + e2b * vt, e1b * bb + e2b, q2)
                return (new_carry, y_t)
            ks = jnp.transpose(k, (1, 0, 2))
            vs = jnp.transpose(v, (1, 0, 2))
            _, ys = jax.lax.scan(step, (aa, bb, pp), (ks, vs))
            return jnp.transpose(ys, (1, 0, 2))
        key = jax.random.key(seed)
        k1, k2, k3, k4 = jax.random.split(key, 4)
        B, T, C = (8, 128, 256)
        return {'batch_size': B, 'seq_len': T, 'embedding_dim': C, 'time_decay': jax.random.normal(k1, (C,), dtype=jnp.float32), 'time_first': jax.random.normal(k2, (C,), dtype=jnp.float32), 'k': jax.random.normal(k3, (B, T, C), dtype=jnp.float32), 'v': jax.random.normal(k4, (B, T, C), dtype=jnp.float32)}
    _L1_xattn_all = _L1_xattn_setup()
    _L1_xattn_in = {k: v for k, v in _L1_xattn_all.items() if k in ('time_decay', 'time_first')}
    del _L1_xattn_all

    def _L1_ffn_setup():
        import jax, jax.numpy as jnp
        import numpy as np
        E = 8
        TOP_K = 2
        D = 256
        DFF = 176
        DFF_S = 352
        B, S = (2, 256)
        key = jax.random.key(seed)
        ks = jax.random.split(key, 8)
        sc = 0.02
        return {'hidden_states': jax.random.normal(ks[0], (B, S, D), jnp.float32), 'gate_weight': jax.random.normal(ks[1], (E, D), jnp.float32) * sc, 'w_gate': jax.random.normal(ks[2], (E, DFF, D), jnp.float32) * sc, 'w_up': jax.random.normal(ks[3], (E, DFF, D), jnp.float32) * sc, 'w_down': jax.random.normal(ks[4], (E, D, DFF), jnp.float32) * sc, 'w_shared_gate': jax.random.normal(ks[5], (DFF_S, D), jnp.float32) * sc, 'w_shared_up': jax.random.normal(ks[6], (DFF_S, D), jnp.float32) * sc, 'w_shared_down': jax.random.normal(ks[7], (D, DFF_S), jnp.float32) * sc}
    _L1_ffn_all = _L1_ffn_setup()
    _L1_ffn_in = {k: v for k, v in _L1_ffn_all.items() if k in ('gate_weight', 'w_gate', 'w_up', 'w_down', 'w_shared_gate', 'w_shared_up', 'w_shared_down')}
    del _L1_ffn_all
    return {'x': x, 'ctx_2048': ctx_2048, 'g_xattn': g_xattn, 'g_ffn': g_ffn, 'L0_xattn_ssm_kernel': _L0_xattn_in['ssm_kernel'], 'L0_xattn_D': _L0_xattn_in['D'], 'L0_ffn_w_gate': _L0_ffn_in['w_gate'], 'L0_ffn_w_shared_up': _L0_ffn_in['w_shared_up'], 'L0_ffn_w_shared_down': _L0_ffn_in['w_shared_down'], 'L0_ffn_w_up': _L0_ffn_in['w_up'], 'L0_ffn_w_down': _L0_ffn_in['w_down'], 'L1_xattn_time_decay': _L1_xattn_in['time_decay'], 'L1_xattn_time_first': _L1_xattn_in['time_first'], 'L1_ffn_gate_weight': _L1_ffn_in['gate_weight'], 'L1_ffn_w_gate': _L1_ffn_in['w_gate'], 'L1_ffn_w_up': _L1_ffn_in['w_up'], 'L1_ffn_w_down': _L1_ffn_in['w_down'], 'L1_ffn_w_shared_gate': _L1_ffn_in['w_shared_gate'], 'L1_ffn_w_shared_up': _L1_ffn_in['w_shared_up'], 'L1_ffn_w_shared_down': _L1_ffn_in['w_shared_down']}

def reference(x, ctx_2048, g_xattn, g_ffn, L0_xattn_ssm_kernel, L0_xattn_D, L0_ffn_w_gate, L0_ffn_w_shared_up, L0_ffn_w_shared_down, L0_ffn_w_up, L0_ffn_w_down, L1_xattn_time_decay, L1_xattn_time_first, L1_ffn_gate_weight, L1_ffn_w_gate, L1_ffn_w_up, L1_ffn_w_down, L1_ffn_w_shared_gate, L1_ffn_w_shared_up, L1_ffn_w_shared_down):
    import jax
    import jax.numpy as jnp

    def _L0_xattn_ref(k, v, q, ssm_kernel, D, head_dim):
        import jax, jax.numpy as jnp
        import numpy as np
        B, HD, L = k.shape
        H = HD // head_dim
        fft_size = 2 * L
        k_ = k.reshape(B, H, head_dim, L)
        v_ = v.reshape(B, H, head_dim, L)
        q_ = q.reshape(B, H, head_dim, L)
        kv = jnp.einsum('bhil,bhjl->bijhl', k_, v_)
        kv_f = jnp.fft.rfft(kv, n=fft_size)
        kernel_f = jnp.fft.rfft(ssm_kernel, n=fft_size)
        y = jnp.fft.irfft(kv_f * kernel_f, n=fft_size)[..., :L]
        out = y + kv * D[None, None, None, :, None]
        out = jnp.einsum('bijhl,bhil->bjhl', out, q_)
        out = jnp.transpose(out, (0, 2, 1, 3)).reshape(B, H * head_dim, L)
        return out.astype(k.dtype)

    def _L0_ffn_ref(x, w_gate, w_shared_up, w_shared_down, w_up, w_down):
        import jax, jax.numpy as jnp
        import numpy as np
        TOPK = 6
        CAP = 128
        ROUTE_SCALE = 1.0
        B, T, C = x.shape
        E = w_gate.shape[1]
        x_flat = x.reshape(-1, C)
        N = x_flat.shape[0]
        su = x_flat @ w_shared_up
        y_s, g_s = jnp.split(su, 2, axis=-1)
        shared = jax.nn.silu(g_s) * y_s @ w_shared_down
        scores = jax.nn.sigmoid(x_flat @ w_gate)
        _, topk_idx = jax.lax.top_k(scores, TOPK)
        w = jnp.take_along_axis(scores, topk_idx, axis=-1)
        w = w / w.sum(-1, keepdims=True) * ROUTE_SCALE
        flat_e = topk_idx.reshape(-1)
        oh = jax.nn.one_hot(flat_e, E, dtype=jnp.int32)
        pos = jnp.take_along_axis(jnp.cumsum(oh, axis=0), flat_e[:, None], axis=1)[:, 0] - 1
        valid = pos < CAP
        pos_c = jnp.where(valid, pos, CAP - 1)
        token_ids = jnp.repeat(jnp.arange(N), TOPK)
        x_disp = jnp.zeros((E, CAP, C), x.dtype).at[flat_e, pos].set(x_flat[token_ids], mode='drop')
        up = jnp.einsum('ecd,edh->ech', x_disp, w_up)
        g_r, v_r = jnp.split(up, 2, axis=-1)
        h_r = jax.nn.silu(g_r) * v_r
        out_r = jnp.einsum('ech,ehd->ecd', h_r, w_down)
        y_ts = out_r[flat_e, pos_c]
        y_ts = jnp.where(valid[:, None], y_ts, 0.0)
        routed = (y_ts.reshape(N, TOPK, C) * w[:, :, None]).sum(axis=1)
        return (shared + routed).reshape(B, T, C)

    def _L1_xattn_ref(batch_size, seq_len, embedding_dim, time_decay, time_first, k, v):
        import jax, jax.numpy as jnp
        import numpy as np

        def _wkv(time_decay, time_first, k, v):
            w = -jnp.exp(time_decay)
            u = time_first
            B, T, C = k.shape
            aa = jnp.zeros((B, C), dtype=k.dtype)
            bb = jnp.zeros((B, C), dtype=k.dtype)
            pp = jnp.full((B, C), -1e+38, dtype=k.dtype)

            def step(carry, kv_t):
                aa, bb, pp = carry
                kt, vt = kv_t
                ww = u + kt
                q = jnp.maximum(pp, ww)
                e1 = jnp.exp(pp - q)
                e2 = jnp.exp(ww - q)
                y_t = (e1 * aa + e2 * vt) / (e1 * bb + e2)
                ww2 = pp + w
                q2 = jnp.maximum(ww2, kt)
                e1b = jnp.exp(ww2 - q2)
                e2b = jnp.exp(kt - q2)
                new_carry = (e1b * aa + e2b * vt, e1b * bb + e2b, q2)
                return (new_carry, y_t)
            ks = jnp.transpose(k, (1, 0, 2))
            vs = jnp.transpose(v, (1, 0, 2))
            _, ys = jax.lax.scan(step, (aa, bb, pp), (ks, vs))
            return jnp.transpose(ys, (1, 0, 2))
        assert seq_len <= 128
        return _wkv(time_decay, time_first, k, v)

    def _L1_ffn_ref(hidden_states, gate_weight, w_gate, w_up, w_down, w_shared_gate, w_shared_up, w_shared_down):
        import jax, jax.numpy as jnp
        import numpy as np
        E = 8
        TOP_K = 2
        D = 256
        DFF = 176
        DFF_S = 352
        B, S = (2, 256)
        orig_shape = hidden_states.shape
        x = hidden_states.reshape(-1, orig_shape[-1])
        logits = x @ gate_weight.T
        scores = jax.nn.softmax(logits, axis=-1)
        topk_w, topk_idx = jax.lax.top_k(scores, TOP_K)
        topk_w = topk_w / jnp.sum(topk_w, axis=-1, keepdims=True)
        topk_w = jax.lax.stop_gradient(topk_w)
        topk_idx = jax.lax.stop_gradient(topk_idx)
        combine = jnp.einsum('tk,tke->te', topk_w, jax.nn.one_hot(topk_idx, E, dtype=x.dtype))
        g = jnp.einsum('td,efd->etf', x, w_gate)
        u = jnp.einsum('td,efd->etf', x, w_up)
        h = jax.nn.silu(g) * u
        expert_out = jnp.einsum('etf,edf->etd', h, w_down)
        y = jnp.einsum('etd,te->td', expert_out, combine)
        sh = jax.nn.silu(x @ w_shared_gate.T) * (x @ w_shared_up.T)
        y = y + sh @ w_shared_down.T
        return y.reshape(orig_shape)
    x = x + jnp.tanh(g_xattn[0]) * _L0_xattn_ref(ctx_2048, ctx_2048, _layernorm(x, axis=-1), L0_xattn_ssm_kernel, L0_xattn_D, 8)
    x = x + jnp.tanh(g_ffn[0]) * _L0_ffn_ref(_layernorm(x, axis=-1), L0_ffn_w_gate, L0_ffn_w_shared_up, L0_ffn_w_shared_down, L0_ffn_w_up, L0_ffn_w_down)
    x = x + jnp.tanh(g_xattn[1]) * _L1_xattn_ref(8, 128, 256, L1_xattn_time_decay, L1_xattn_time_first, _layernorm(x, axis=-1), ctx_2048)
    x = x + jnp.tanh(g_ffn[1]) * _L1_ffn_ref(_layernorm(x, axis=-1), L1_ffn_gate_weight, L1_ffn_w_gate, L1_ffn_w_up, L1_ffn_w_down, L1_ffn_w_shared_gate, L1_ffn_w_shared_up, L1_ffn_w_shared_down)
    return x

_drawn_inputs = setup_inputs


def setup_inputs(seed=0):
    import zlib

    import numpy as np

    out = dict(_drawn_inputs(seed))
    spreads = {'g_ffn': (-1.0, 0.6)}
    factors = {'L0_ffn_w_gate': 43.216,
     'L0_ffn_w_shared_up': 33.351,
     'L0_ffn_w_shared_down': 32.804,
     'L0_ffn_w_up': 46.915,
     'L0_ffn_w_down': 46.721,
     'L1_xattn_time_decay': 176.548,
     'L1_xattn_time_first': 34.277,
     'L1_ffn_gate_weight': 8.0,
     'L1_ffn_w_gate': 8.0,
     'L1_ffn_w_up': 8.0,
     'L1_ffn_w_down': 8.0,
     'L1_ffn_w_shared_gate': 8.0,
     'L1_ffn_w_shared_up': 8.0,
     'L1_ffn_w_shared_down': 8.0}
    for name, (base, spread) in spreads.items():
        noise = np.random.default_rng([zlib.crc32(name.encode()), seed]).standard_normal(out[name].shape)
        drawn = base * np.exp(spread * noise) if base else spread * noise
        out[name] = jnp.asarray(drawn.astype(out[name].dtype))
    for name, factor in factors.items():
        out[name] = (out[name] * factor).astype(out[name].dtype)
    return out
```

```python
from contextlib import ExitStack

import concourse.bass as bass
from concourse import mybir

F32 = mybir.dt.float32
F32R = mybir.dt.float32r
BF16 = mybir.dt.bfloat16
U32 = mybir.dt.uint32
I32 = mybir.dt.int32
ALU = mybir.AluOpType
ACT = mybir.ActivationFunctionType
AX = mybir.AxisListType

P = 128
B, R, C = 8, 128, 256
NT = C // P
HEADS, HD = 16, 8
HG = 4
NHG = HEADS // HG
KW = HD * HD
BLK = NT * HG
LN_EPS = 1e-5

E0, H0, TOP0, CAP0, HS0 = 64, 32, 6, 128, 64
CH0 = 4
CE0 = E0 // CH0
CF0 = CE0 * H0
UW0 = E0 * 2 * H0 + 2 * HS0
KT0 = CF0 // P
NK0 = CH0 * KT0 + 1
NCH = CH0 + 1

E1, H1, TOP1, HS1 = 8, 176, 2, 352
CF1 = 2 * H1
UW1 = NCH * 2 * CF1
KT1 = (CF1 + P - 1) // P
CP1 = KT1 * P
NK1 = NCH * KT1

SL0 = 4
PC0 = (NT * UW0 + NK0 * C) // (NHG * SL0)
PCU1 = NT * UW1 // B
SL1 = 2
ND1 = 4
PCD1 = NK1 * C // ND1

RT0, RT1 = 11, 11
WK = 15
N_SMALL = 6


def build(nc, x, ctx_t, ctx_rev, conv_pad, conv_d, gates, w0, w_gate0, w1, w_gate1, decay, first, out):
    es = ExitStack()
    with es:
        def sb(name, shape, dt=F32, stack=es):
            return stack.enter_context(nc.sbuf_tensor(name, shape, dt))

        def pb(name, shape):
            return es.enter_context(nc.psum_tensor(name, shape, F32))

        def sem(name):
            return es.enter_context(nc.semaphore(name))

        xs = sb("xs", [P, B, C])
        w0_hi = sb("w0_hi", [P, NT * UW0 + NK0 * C], F32R)
        w0_lo = sb("w0_lo", [P, NT * UW0 + NK0 * C], F32R)
        stage1 = sb("stage1", [P, SL1, max(PCU1, PCD1)])
        ident = sb("ident", [P, P])
        anti = sb("anti", [P, P])
        tri = sb("tri", [P, P], BF16)
        ones = sb("ones", [P, P], BF16)
        iota0 = sb("iota0", [P, E0])
        iota_i = sb("iota_i", [P, E0], I32)
        nhalf = sb("nhalf", [P, B])
        db = sb("db", [P, HEADS])
        gates_sb = sb("gates_sb", [P, 4])
        gt = sb("gt", [P, 4])
        wg0 = sb("wg0", [P, NT, E0])
        wg1 = sb("wg1", [P, NT, E1])
        td = sb("td", [P, NT])
        tdc = sb("tdc", [P, NT])
        etd = sb("etd", [P, NT])
        dc = sb("dc", [P, NT])
        fs = sb("fs", [P, NT])
        umax = sb("umax", [P, NT])
        umin = sb("umin", [P, NT])
        c1 = sb("c1", [P, NT])
        c2 = sb("c2", [P, NT])
        bstq = sb("bstq", [P, B, 6])
        mvq = sb("mvq", [P, B, 2])
        veq = sb("veq", [P, B])
        rsq = sb("rsq", [P, B])
        bst = sb("bst", [P, 6])
        mv = sb("mv", [P, 2])
        ve = sb("ve", [P, 1])
        rs = sb("rs", [P, 1])
        xn = sb("xn", [P, C])

        a_stage = ExitStack()
        tz = sb("tz", [P, 2, HG, 2 * P], stack=a_stage)
        z = sb("z", [P, NT, HG, B * KW], stack=a_stage)
        qt = sb("qt", [P, NT, B, R], stack=a_stage)
        prod = sb("prod", [P, 4, B * KW], stack=a_stage)
        oc = sb("oc", [P, NT, B, R], stack=a_stage)
        cr = sb("cr", [P, NT, B, R], stack=a_stage)
        qn = oc[:].rearrange("p t b r -> p (t b r)").rearrange("p (b c) -> p b c", b=B)
        stage0 = sb("stage0", [P, SL0, PC0], stack=a_stage)
        a_stage.close()

        w1u_hi = sb("w1u_hi", [P, NT * UW1], F32R)
        w1u_lo = sb("w1u_lo", [P, NT * UW1], F32R)
        ct = sb("ct", [P, NT, B, R])
        sil = sb("sil", [P, CF0])
        av = sb("av", [P, CF0])
        hw = sb("hw", [P, CF0])
        hT_hi = sb("hT_hi", [P, KT0 * P], F32R)
        hT_lo = sb("hT_lo", [P, KT0 * P], F32R)
        ek = sb("ek", [P, NT, R])
        ev = sb("ev", [P, NT, R])
        sa = sb("sa", [P, NT, R + 1])
        sb_ = sb("sb_", [P, NT, R + 1])
        xn2 = sb("xn2", [P, C])
        yt = xn2[:, :].rearrange("p (t r) -> p t r", t=NT)
        eq = sb("eq", [P, TOP0, E0])
        xT = sb("xT", [P, NT, R])
        xT_hi = sb("xT_hi", [P, NT, R], F32R)
        xT_lo = sb("xT_lo", [P, NT, R], F32R)
        es0 = sb("es0", [P, E0])
        sc = sb("sc", [P, E0])
        v8 = sb("v8", [P, 8])
        i8 = sb("i8", [P, 8], U32)
        f8 = sb("f8", [P, 8])
        mask = sb("mask", [P, E0])
        maskb = sb("maskb", [P, E0], BF16)
        run = sb("run", [P, E0], BF16)
        den = sb("den", [P, 1])
        rden = sb("rden", [P, 1])
        msc = sb("msc", [P, E0])
        g = sb("g", [P, E0])
        nmx = sb("nmx", [P, 1])
        bst2 = sb("bst2", [P, 6])
        mv2 = sb("mv2", [P, 2])
        ve2 = sb("ve2", [P, 1])
        rs2 = sb("rs2", [P, 1])

        U = [pb(f"U{i}", [P, 2, 512]) for i in range(2)]
        HT = pb("HT", [P, 512])
        DN = pb("DN", [P, 512])
        M0 = pb("M0", [P, 512])
        M1 = pb("M1", [P, 512])
        Y = [U[0][:, 0, :], U[0][:, 1, :], U[1][:, 0, :], U[1][:, 1, :]]
        M = [M0, M1]
        XT, LG, PS = M0[:, 0:C], M0[:, C:C + E0], M0[:, C + E0:C + 2 * E0]
        LG1 = M0[:, C:C + E1]

        def up0(part, t, a, b):
            return part[:, t * UW0 + a:t * UW0 + b]

        def down0(part, k):
            return part[:, NT * UW0 + k * C:NT * UW0 + (k + 1) * C]

        def up1(part, t, a, b):
            return part[:, t * UW1 + a:t * UW1 + b]

        D1_AT = NK1 * C
        def down1(low, k):
            return w0_hi[:, low * D1_AT + k * C:low * D1_AT + (k + 1) * C]

        ctx_in, x_in, small_in, ct_in = sem("ctx_in"), sem("x_in"), sem("small_in"), sem("ct_in")
        toep_in = [sem(f"toep_in{i}") for i in range(2)]
        stage0_in = [sem(f"stage0_in{i}") for i in range(SL0)]
        stage1_in = [sem(f"stage1_in{i}") for i in range(SL1)]
        out_done = sem("out_done")
        memset_ok, const_ok, iota_ok = sem("memset_ok"), sem("const_ok"), sem("iota_ok")
        passed_dve, passed_pe = sem("passed_dve"), sem("passed_pe")
        setup_dve, setup_act = sem("setup_dve"), sem("setup_act")
        s0_hi, s0_lo = sem("s0_hi"), sem("s0_lo")
        s1_hi, s1_lo = sem("s1_hi"), sem("s1_lo")
        qstep, qvar_ok, qrstd_ok, qn_ok = sem("qstep"), sem("qvar_ok"), sem("qrstd_ok"), sem("qn_ok")
        qT_ps, qT_ok = sem("qT_ps"), sem("qT_ok")
        toep_ok, z_dve, z_pool = sem("toep_ok"), sem("z_dve"), sem("z_pool")
        conv_ps, prod_ok, oc_ok = sem("conv_ps"), sem("prod_ok"), sem("oc_ok")
        oT_ps, x1_ok = sem("oT_ps"), sem("x1_ok")
        ln_step, var_ok, rstd_ok, xn_ok = sem("ln_step"), sem("var_ok"), sem("rstd_ok"), sem("xn_ok")
        xT_ps, xT_ok, xT_hi_ok, xT_lo_ok = sem("xT_ps"), sem("xT_ok"), sem("xT_hi_ok"), sem("xT_lo_ok")
        lg_ps, exp_ok, route, mask_ok = sem("lg_ps"), sem("exp_ok"), sem("route"), sem("mask_ok")
        nmx_ok = sem("nmx_ok")
        pos_ps, g_ok, run_ok = sem("pos_ps"), sem("g_ok"), sem("run_ok")
        up_ps, sil_ok, av_ok, hw_ok = sem("up_ps"), sem("sil_ok"), sem("av_ok"), sem("hw_ok")
        hT_ps, hT_hi_ok, hT_lo_ok, down_ps = sem("hT_ps"), sem("hT_hi_ok"), sem("hT_lo_ok"), sem("down_ps")
        x2_ok, x4_ok, pad_ok = sem("x2_ok"), sem("x4_ok"), sem("pad_ok")
        ln2_step, var2_ok, rstd2_ok, xn2_ok = sem("ln2_step"), sem("var2_ok"), sem("rstd2_ok"), sem("xn2_ok")
        kT_ps, ek_ok, wk_step, y_ok, yT_ps, x3_ok = (sem("kT_ps"), sem("ek_ok"), sem("wk_step"), sem("y_ok"),
                                                      sem("yT_ps"), sem("x3_ok"))

        block = es.enter_context(nc.Block())

        @block.sync
        def _(sp):
            def toeplitz(hg, slot):
                src = bass.AP(conv_pad.tensor, hg * (HG * 3 * P),
                                                            [[1, P], [3 * P, HG], [1, 2 * P]])
                sp.dma_start(tz[:, slot], src).then_inc(toep_in[slot], 16)

            def pieces0(grp, again):
                for k in range(SL0):
                    if again:
                        sp.wait_ge(s0_lo, SL0 * (grp - 1) + k + 1)
                    sp.dma_start(stage0[:, k, :], w0[:, bass.ds((grp * SL0 + k) * PC0, PC0)])\
                        .then_inc(stage0_in[k], 16)

            sp.dma_start(cr[:], ctx_rev).then_inc(ctx_in, 16)
            toeplitz(0, 0)
            sp.dma_start(xs[:], x.rearrange("b r c -> r b c")).then_inc(x_in, 16)
            toeplitz(1, 1)
            pieces0(0, False)
            for grp in range(1, NHG - 1):
                pieces0(grp, True)
                sp.wait_ge(conv_ps, BLK * grp)
                toeplitz(grp + 1, (grp + 1) % 2)
            pieces0(NHG - 1, True)
            sp.wait_ge(x1_ok, B)
            sp.wait_ge(s0_lo, NHG * SL0)
            sp.dma_start(ct[:], ctx_t).then_inc(ct_in, 16)
            sp.dma_start(stage1[:, 0, 0:PCU1], w1[:, 0:PCU1]).then_inc(stage1_in[0], 16)
            with sp.Fori(1, B) as b:
                sp.wait_ge(s1_lo, b)
                sp.dma_start(stage1[:, 0, 0:PCU1], w1[:, bass.ds(b * PCU1, PCU1)]).then_inc(stage1_in[0], 16)
            for k in range(ND1):
                if k % SL1 == 0:
                    sp.wait_ge(s1_lo, B + max(k - 1, 0))
                elif k > SL1:
                    sp.wait_ge(s1_lo, B + k - 1)
                at = NT * UW1 + k * PCD1
                sp.dma_start(stage1[:, k % SL1, 0:PCD1], w1[:, at:at + PCD1]).then_inc(stage1_in[k % SL1], 16)
            with sp.Fori(0, B) as b:
                sp.wait_ge(x4_ok, b + 1)
                sp.dma_start(out[bass.ds(b, 1)].rearrange("b r c -> r (b c)"),
                             xs[:, bass.ds(b, 1), :].rearrange("r b c -> r (b c)")).then_inc(out_done, 16)
            sp.wait_ge(out_done, 16 * B)

        @block.gpsimd
        def _(pool):
            pool.memset(ident[:], 0.0).then_inc(memset_ok, 1)
            pool.memset(anti[:], 0.0).then_inc(memset_ok, 1)
            pool.memset(tri[:], 1.0).then_inc(memset_ok, 1)
            pool.memset(ones[:], 1.0).then_inc(const_ok, 1)
            pool.memset(nhalf[:], -0.5).then_inc(const_ok, 1)
            pool.iota(iota_i[:], [[1, E0]], base=0, channel_multiplier=0).then_inc(iota_ok, 1)
            pool.wait_ge(memset_ok, 3)
            pool.affine_select(out=ident[:], in_=ident[:], compare_op=ALU.not_equal, fill=1.0, base=0,
                               pattern=[[-1, P]], channel_multiplier=1).then_inc(const_ok, 1)
            pool.affine_select(out=anti[:], in_=anti[:], compare_op=ALU.not_equal, fill=1.0, base=-(P - 1),
                               pattern=[[1, P]], channel_multiplier=1).then_inc(const_ok, 1)
            pool.affine_select(out=tri[:], in_=tri[:], compare_op=ALU.is_gt, fill=0.0, base=0,
                               pattern=[[1, P]], channel_multiplier=-1).then_inc(const_ok, 1)
            pool.wait_ge(const_ok, 5)
            pool.wait_ge(qvar_ok, 1)
            pool.tensor_tensor(rsq[:], veq[:], nhalf[:], ALU.pow).then_inc(qrstd_ok, 1)

            pool.wait_ge(ctx_in, 16)

            def z_of(hg, h):
                rows = cr[:, 1, :, bass.ds(hg * (HG * HD) + h * HD, HD)]
                pool.tensor_tensor(z[:, 1, h, :].rearrange("p (b i j) -> p b i j", b=B, i=HD),
                                   rows.unsqueeze(3).to_broadcast([P, B, HD, HD]),
                                   rows.unsqueeze(2).to_broadcast([P, B, HD, HD]), ALU.mult).then_inc(z_pool, 1)

            with pool.Fori(0, NHG) as hg:
                for h in range(HG):
                    z_of(hg, h)
                for k in range(SL0):
                    pool.wait_ge(s0_hi, SL0 * hg + k + 1)
                    at = bass.ds((hg * SL0 + k) * PC0, PC0)
                    pool.tensor_tensor(w0_lo[:, at], stage0[:, k, :], w0_hi[:, at].bitcast(F32),
                                       ALU.subtract).then_inc(s0_lo, 1)
                pool.wait_ge(conv_ps, BLK * (hg + 1))

            def rstd(n):
                pool.wait_ge(var_ok, n + 1)
                pool.tensor_tensor(rs[:], ve[:], nhalf[:, 0:1], ALU.pow).then_inc(rstd_ok, 1)

            def rstd2(b):
                pool.wait_ge(var2_ok, b + 1)
                pool.tensor_tensor(rs2[:], ve2[:], nhalf[:, 0:1], ALU.pow).then_inc(rstd2_ok, 1)

            def weigh(b, c):
                pool.wait_ge(av_ok, NCH * b + c + 1)
                if c > 0:
                    pool.wait_ge(hT_ps, NCH * b + c)
                grp = g[:, c * CE0:(c + 1) * CE0].unsqueeze(2).to_broadcast([P, CE0, H0])
                pool.tensor_tensor(hw[:].rearrange("p (e h) -> p e h", e=CE0),
                                   av[:].rearrange("p (e h) -> p e h", e=CE0), grp, ALU.mult)\
                    .then_inc(hw_ok, 1)

            def tile(b, last):
                if not isinstance(b, int):
                    rstd2(b - 1)
                pool.wait_ge(g_ok, b + 1)
                for c in range(CH0):
                    weigh(b, c)
                if not last:
                    rstd(b + 1)
                pool.wait_ge(s1_hi, b + 1)
                at = bass.ds(b * PCU1, PCU1)
                pool.tensor_tensor(w1u_lo[:, at], stage1[:, 0, 0:PCU1], w1u_hi[:, at].bitcast(F32),
                                   ALU.subtract).then_inc(s1_lo, 1)
                pool.wait_ge(hT_ps, NCH * b + CH0)

            rstd(0)
            tile(0, False)
            with pool.Fori(1, B - 1) as b:
                tile(b, False)
            rstd2(B - 2)
            pool.wait_ge(g_ok, B)
            for c in range(CH0):
                weigh(B - 1, c)
            rstd(B)
            at = bass.ds((B - 1) * PCU1, PCU1)
            pool.wait_ge(s1_hi, B)
            pool.tensor_tensor(w1u_lo[:, at], stage1[:, 0, 0:PCU1], w1u_hi[:, at].bitcast(F32),
                               ALU.subtract).then_inc(s1_lo, 1)
            rstd2(B - 1)
            for k in range(ND1):
                pool.wait_ge(s1_hi, B + k + 1)
                at = k * PCD1
                pool.tensor_tensor(w0_hi[:, D1_AT + at:D1_AT + at + PCD1], stage1[:, k % SL1, 0:PCD1],
                                   w0_hi[:, at:at + PCD1].bitcast(F32), ALU.subtract).then_inc(s1_lo, 1)
            with pool.Fori(1, B) as b:
                rstd(b + B)

        @block.scalar
        def _(act):
            act.dma_start(db[:], conv_d.to_broadcast([P, HEADS])).then_inc(small_in, 16)
            act.dma_start(gates_sb[:], gates.to_broadcast([P, 4])).then_inc(small_in, 16)
            act.dma_start(td[:], decay).then_inc(small_in, 16)
            act.dma_start(fs[:], first).then_inc(small_in, 16)
            act.dma_start(wg0[:], w_gate0).then_inc(small_in, 16)
            act.dma_start(wg1[:], w_gate1).then_inc(small_in, 16)
            act.wait_ge(small_in, 16 * N_SMALL)
            act.activation(gt[:], gates_sb[:], ACT.Tanh).then_inc(setup_act, 1)
            act.wait_ge(setup_dve, 4)
            act.activation(etd[:], tdc[:], ACT.Exp).then_inc(setup_act, 1)
            act.wait_ge(setup_act, 2)
            act.activation(dc[:], etd[:], ACT.Exp, scale=-1.0).then_inc(setup_act, 1)
            act.activation(c1[:], umax[:], ACT.Exp, scale=-1.0).then_inc(setup_act, 1)
            act.activation(c2[:], umin[:], ACT.Exp).then_inc(setup_act, 1)
            for b in range(B):
                act.wait_ge(qT_ps, b + 1)
                act.activation(qt[:, :, b, :], M[b % 2][:, 0:C].rearrange("p (t r) -> p t r", t=NT),
                               ACT.Copy).then_inc(qT_ok, 1)
            with act.Fori(0, NHG) as grp:
                for k in range(SL0):
                    act.wait_ge(stage0_in[k], 16 * (grp + 1))
                    act.activation(w0_hi[:, bass.ds((grp * SL0 + k) * PC0, PC0)], stage0[:, k, :],
                                   ACT.Copy).then_inc(s0_hi, 1)

            def turned(n):
                act.wait_ge(xT_ps, n + 1)
                act.activation(xT[:].rearrange("p t r -> p (t r)"), XT, ACT.Copy).then_inc(xT_ok, 1)
                act.wait_ge(xT_ok, n + 1)
                act.activation(xT_hi[:], xT[:], ACT.Copy).then_inc(xT_hi_ok, 1)

            def exp0(b):
                act.wait_ge(lg_ps, b + 1)
                act.activation(es0[:], LG, ACT.Exp, scale=-1.0).then_inc(exp_ok, 1)

            def silu(n, c, src, width, split):
                act.wait_ge(up_ps, NCH * n + c + 1)
                if c > 0:
                    act.wait_ge(av_ok, NCH * n + c)
                dst = sil[:, 0:width]
                if split:
                    dst = dst.rearrange("p (n w) -> p n w", n=split)
                act.activation(dst, src, ACT.Silu).then_inc(sil_ok, 1)

            def high(n, c, rows, width):
                act.wait_ge(hT_ps, NCH * n + c + 1)
                if c > 0:
                    act.wait_ge(down_ps, NCH * n + c)
                act.activation(hT_hi[0:rows, 0:width], HT[0:rows, 0:width], ACT.Copy).then_inc(hT_hi_ok, 1)

            def silu0(b, c):
                if c < CH0:
                    src = U[c % 2][:].rearrange("p n (e w) -> p (n e) w", w=2 * H0)[:, :, 0:H0]
                    silu(b, c, src, CF0, CE0)
                else:
                    silu(b, c, U[0][:, 0, HS0:2 * HS0], HS0, 0)

            def high0(b, c):
                high(b, c, P if c < CH0 else HS0, CF0 if c < CH0 else P)

            def split1(b):
                act.wait_ge(stage1_in[0], 16 * (b + 1))
                act.activation(w1u_hi[:, bass.ds(b * PCU1, PCU1)], stage1[:, 0, 0:PCU1], ACT.Copy)\
                    .then_inc(s1_hi, 1)

            def ek_of(b):
                act.wait_ge(kT_ps, b + 1)
                act.activation(ek[:].rearrange("p t r -> p (t r)"), M1[:, 0:C], ACT.Exp).then_inc(ek_ok, 1)

            def tile0(b, first, last):
                silu0(b, 0)
                silu0(b, 1)
                high0(b, 0)
                if not first:
                    ek_of(b - 1)
                silu0(b, 2)
                high0(b, 1)
                silu0(b, 3)
                high0(b, 2)
                silu0(b, 4)
                high0(b, 3)
                turned(b + 1)
                if not last:
                    exp0(b + 1)
                else:
                    exp1(0)
                high0(b, 4)
                split1(b)
                act.wait_ge(down_ps, NCH * (b + 1))
                act.wait_ge(av_ok, NCH * (b + 1))

            def exp1(b):
                act.wait_ge(nmx_ok, b + 1)
                act.activation(es0[:, 0:E1], LG1, ACT.Exp, bias=nmx[:, 0:1]).then_inc(exp_ok, 1)

            turned(0)
            exp0(0)
            tile0(0, True, False)
            with act.Fori(1, B - 1) as b:
                tile0(b, False, False)
            tile0(B - 1, False, True)
            ek_of(B - 1)
            for k in range(ND1):
                act.wait_ge(stage1_in[k % SL1], (16 * (B + k // SL1 + 1)) if k % SL1 == 0 else 16 * (k // SL1 + 1))
                act.activation(w0_hi[:, k * PCD1:(k + 1) * PCD1], stage1[:, k % SL1, 0:PCD1], ACT.Copy)\
                    .then_inc(s1_hi, 1)

            def tile1(b, last):
                n = b + B
                for c in range(NCH):
                    silu(n, c, U[c % 2][:, 0, 0:CF1], CF1, 0)
                    if c > 0:
                        high(n, c - 1, P, CP1)
                if not last:
                    turned(n + 1)
                    exp1(b + 1)
                high(n, NCH - 1, P, CP1)
                act.wait_ge(down_ps, NCH * (n + 1))
                act.wait_ge(av_ok, NCH * (n + 1))

            with act.Fori(0, B - 1) as b:
                tile1(b, False)
            tile1(B - 1, True)

        @block.tensor
        def _(pe):
            def turn(dst, src, rows=P):
                return pe.transpose(dst, src, ident[:])

            pe.wait_ge(const_ok, 5)
            for b in range(B):
                pe.wait_ge(qn_ok, b + 1)
                if b >= 2:
                    pe.wait_ge(qT_ok, b - 1)
                for t in range(NT):
                    mm = turn(M[b % 2][:, t * P:(t + 1) * P], qn[:, b, t * P:(t + 1) * P])
                mm.then_inc(qT_ps, 1)

            with pe.Fori(0, NHG // 2) as i:
                for par in range(2):
                    hg = 2 * i + par
                    for h in range(HG):
                        pe.wait_ge(toep_ok, HG * hg + h + 1)
                        pe.wait_ge(z_dve, HG * hg + h + 1)
                        k = NT * h
                        if k >= 4:
                            pe.wait_ge(prod_ok, BLK * hg + k - 3)
                        pe.matmul(Y[k % 4], tz[:, par, h, 0:P], z[:, 0, h, :], start=True, stop=True)\
                            .then_inc(conv_ps, 1)
                        pe.wait_ge(z_pool, HG * hg + h + 1)
                        k += 1
                        if k >= 4:
                            pe.wait_ge(prod_ok, BLK * hg + k - 3)
                        pe.matmul(Y[k % 4], tz[:, par, h, P:2 * P], z[:, 0, h, :], start=True, stop=False)
                        pe.matmul(Y[k % 4], tz[:, par, h, 0:P], z[:, 1, h, :], start=False, stop=True)\
                            .then_inc(conv_ps, 1)
                    pe.wait_ge(prod_ok, BLK * (hg + 1))

            pe.wait_ge(oc_ok, BLK * NHG)
            for b in range(B):
                if b >= 2:
                    pe.wait_ge(x1_ok, b - 1)
                for t in range(NT):
                    mm = turn(M[b % 2][:, t * P:(t + 1) * P], oc[:, t, b, :])
                mm.then_inc(oT_ps, 1)
            pe.wait_ge(x1_ok, B)
            pe.wait_ge(s0_lo, NHG * SL0)

            def pre(n):
                pe.wait_ge(xn_ok, n + 1)
                for t in range(NT):
                    mm = turn(XT[:, t * P:(t + 1) * P], xn[:, t * P:(t + 1) * P])
                mm.then_inc(xT_ps, 1)

            def logits(n, w, dst):
                pe.wait_ge(xT_ok, n + 1)
                for t in range(NT):
                    mm = pe.matmul(dst, xT[:, t, :], w[:, t, :], start=(t == 0), stop=(t == NT - 1))
                mm.then_inc(lg_ps, 1)

            def places(b):
                pe.wait_ge(mask_ok, b + 1)
                pe.wait_ge(run_ok, b + 1)
                pe.matmul(PS, tri[:], maskb[:], start=True, stop=False)
                pe.matmul(PS, ones[:], run[:], start=False, stop=True).then_inc(pos_ps, 1)

            def up(n, c, dst, cols):
                if c >= 2:
                    pe.wait_ge(av_ok, NCH * n + c - 1)
                if c == 0:
                    pe.wait_ge(xT_hi_ok, n + 1)
                    pe.wait_ge(xT_lo_ok, n + 1)
                parts = [(xT_hi, t, w) for t in range(NT) for w in (0, 1)] + [(xT_lo, t, 0) for t in range(NT)]
                for i, (xp, t, w) in enumerate(parts):
                    for d, col in zip(dst, cols):
                        mm = pe.matmul(d, xp[:, t, :], col(w, t), start=(i == 0), stop=(i == len(parts) - 1))
                mm.then_inc(up_ps, 1)

            def up_0(b, c):
                if c < CH0:
                    dst = [U[c % 2][:, n, :] for n in range(2)]
                    cols = [lambda w, t, a=(2 * c + n) * 512: up0((w0_hi, w0_lo)[w], t, a, a + 512) for n in range(2)]
                else:
                    dst = [U[0][:, 0, 0:2 * HS0]]
                    cols = [lambda w, t: up0((w0_hi, w0_lo)[w], t, UW0 - 2 * HS0, UW0)]
                up(b, c, dst, cols)

            def up_1(b, c):
                dst = [U[c % 2][:, n, 0:CF1] for n in range(2)]
                cols = [lambda w, t, a=(2 * c + n) * CF1: up1((w1u_hi, w1u_lo)[w], t, a, a + CF1) for n in range(2)]
                up(b + B, c, dst, cols)

            def turn_h(n, c, kts, src, rows=P):
                if c > 0:
                    pe.wait_ge(hT_lo_ok, NCH * n + c)
                    pe.sem_inc(passed_pe, 1)
                for k in range(kts):
                    mm = turn(HT[0:rows, k * P:(k + 1) * P], src[:, k * P:k * P + rows])
                mm.then_inc(hT_ps, 1)

            def turn_0(b, c):
                if c < CH0:
                    pe.wait_ge(hw_ok, CH0 * b + c + 1)
                    turn_h(b, c, KT0, hw)
                else:
                    pe.wait_ge(av_ok, NCH * b + c + 1)
                    turn_h(b, c, 1, av, HS0)

            def turn_1(b, c):
                n = b + B
                pe.wait_ge(av_ok, NCH * n + c + 1)
                turn_h(n, c, KT1, hw)

            def down(n, c, kts, w, rows, free):
                pe.wait_ge(hT_lo_ok, NCH * n + c + 1)
                if free:
                    pe.wait_ge(*free)
                for k in range(kts):
                    for i, (h, lo) in enumerate(((hT_hi, 0), (hT_hi, 1), (hT_lo, 0))):
                        mm = pe.matmul(DN[:, 0:C], h[0:rows, k * P:(k + 1) * P], w(lo, c, k)[0:rows],
                                       start=(c == 0 and k == 0 and i == 0),
                                       stop=(c == NCH - 1 and k == kts - 1 and i == 2))
                mm.then_inc(down_ps, 1)

            def w_0(lo, c, k):
                return down0((w0_hi, w0_lo)[lo], c * KT0 + k)

            def w_1(lo, c, k):
                return down1(lo, c * KT1 + k)

            def down_0(b, c, first=False):
                if c < CH0:
                    down(b, c, KT0, w_0, P, (x2_ok, b) if c == 0 and not first else None)
                else:
                    down(b, c, 1, w_0, HS0, None)

            def down_1(b, c, first=False):
                free = None if c > 0 else (x2_ok, B) if first else (x4_ok, b)
                down(b + B, c, KT1, w_1, P, free)

            def kT(b):
                pe.wait_ge(xn2_ok, b + 1)
                for t in range(NT):
                    mm = turn(M1[:, t * P:(t + 1) * P], xn2[:, t * P:(t + 1) * P])
                mm.then_inc(kT_ps, 1)

            def yT(b):
                pe.wait_ge(y_ok, b + 1)
                for t in range(NT):
                    mm = turn(M1[:, t * P:(t + 1) * P], yt[:, t, :])
                mm.then_inc(yT_ps, 1)

            def tile0(b, first, last):
                up_0(b, 0)
                up_0(b, 1)
                turn_0(b, 0)
                if not first:
                    kT(b - 1)
                up_0(b, 2)
                down_0(b, 0, first)
                turn_0(b, 1)
                up_0(b, 3)
                down_0(b, 1)
                turn_0(b, 2)
                if not first:
                    yT(b - 1)
                up_0(b, 4)
                down_0(b, 2)
                turn_0(b, 3)
                pre(b + 1)
                if not last:
                    logits(b + 1, wg0, LG)
                else:
                    logits(b + 1, wg1, LG1)
                down_0(b, 3)
                turn_0(b, 4)
                down_0(b, 4)
                if not last:
                    places(b + 1)

            pre(0)
            logits(0, wg0, LG)
            places(0)
            tile0(0, True, False)
            with pe.Fori(1, B - 1) as b:
                tile0(b, False, False)
            tile0(B - 1, False, True)
            kT(B - 1)
            pe.wait_ge(s1_lo, B)

            def tile1(b, last, first):
                up_1(b, 0)
                for c in range(1, NCH):
                    up_1(b, c)
                    turn_1(b, c - 1)
                    if first and c == 1:
                        yT(B - 1)
                    if c >= 2:
                        if first and c == 2:
                            pe.wait_ge(s1_lo, B + ND1)
                        down_1(b, c - 2, first)
                if not last:
                    pre(b + B + 1)
                    logits(b + B + 1, wg1, LG1)
                down_1(b, NCH - 2)
                turn_1(b, NCH - 1)
                down_1(b, NCH - 1)

            tile1(0, False, True)
            with pe.Fori(1, B - 1) as b:
                tile1(b, False, False)
            tile1(B - 1, True, False)

        @block.vector
        def _(dve):
            def after(ins, s, value):
                ins.then_inc(s, 1)
                dve.wait_ge(s, value)
                dve.sem_inc(passed_dve, 1)

            dve.wait_ge(small_in, 16 * N_SMALL)
            dve.tensor_scalar(umax[:], fs[:], 0.0, None, ALU.max).then_inc(setup_dve, 1)
            dve.tensor_scalar(umin[:], fs[:], 0.0, None, ALU.min).then_inc(setup_dve, 1)
            dve.tensor_scalar(tdc[:], td[:], 80.0, None, ALU.min).then_inc(setup_dve, 1)
            dve.wait_ge(iota_ok, 1)
            dve.tensor_copy(iota0[:], iota_i[:]).then_inc(setup_dve, 1)

            dve.wait_ge(x_in, 16)
            for b in range(B):
                dve.bn_stats(bstq[:, b, :], xs[:, b, :]).then_inc(qstep, 1)
            dve.wait_ge(qstep, B)
            for b in range(B):
                dve.bn_aggr(mvq[:, b, :], bstq[:, b, :]).then_inc(qstep, 1)
            dve.wait_ge(qstep, 2 * B)
            dve.tensor_scalar(veq[:], mvq[:, :, 1], LN_EPS, None, ALU.add).then_inc(qvar_ok, 1)
            dve.wait_ge(qrstd_ok, 1)
            for b in range(B):
                dve.tensor_scalar(qn[:, b, :], xs[:, b, :], mvq[:, b, 0:1], rsq[:, b:b + 1],
                                  ALU.subtract, ALU.mult).then_inc(qn_ok, 1)

            dve.wait_ge(const_ok, 5)
            dve.wait_ge(ctx_in, 16)
            with dve.Fori(0, NHG // 2) as i:
                for par in range(2):
                    hg = 2 * i + par
                    dve.wait_ge(toep_in[par], 16 * (i + 1))
                    for h in range(HG):
                        rows = cr[:, 0, :, bass.ds(hg * (HG * HD) + h * HD, HD)]
                        dve.tensor_tensor(z[:, 0, h, :].rearrange("p (b i j) -> p b i j", b=B, i=HD),
                                          rows.unsqueeze(3).to_broadcast([P, B, HD, HD]),
                                          rows.unsqueeze(2).to_broadcast([P, B, HD, HD]), ALU.mult)\
                            .then_inc(z_dve, 1)
                        dve.scalar_tensor_tensor(out=tz[:, par, h, 0:P], in0=anti[:],
                                                 scalar=db[:, bass.ds(hg * HG + h, 1)], in1=tz[:, par, h, 0:P],
                                                 op0=ALU.mult, op1=ALU.add).then_inc(toep_ok, 1)
                    dve.wait_ge(qT_ok, B)

                    def sum_rows(k):
                        h, t = k // NT, k % NT
                        dve.wait_ge(prod_ok, BLK * hg + k + 1)
                        dve.tensor_reduce(oc[:, t, :, bass.ds(hg * (HG * HD) + h * HD, HD)],
                                          prod[:, k % 4, :].rearrange("p (b i j) -> p b j i", b=B, i=HD),
                                          AX.X, ALU.add).then_inc(oc_ok, 1)

                    for k in range(BLK):
                        h, t = k // NT, k % NT
                        dve.wait_ge(conv_ps, BLK * hg + k + 1)
                        if k >= 4:
                            dve.wait_ge(oc_ok, BLK * hg + k - 3)
                        q = qt[:, t, :, bass.ds(hg * (HG * HD) + h * HD, HD)]
                        dve.tensor_tensor(prod[:, k % 4, :].rearrange("p (b i j) -> p b i j", b=B, i=HD),
                                          Y[k % 4].rearrange("p (b i j) -> p b i j", b=B, i=HD),
                                          q.unsqueeze(3).to_broadcast([P, B, HD, HD]), ALU.mult)\
                            .then_inc(prod_ok, 1)
                        if k > 0:
                            sum_rows(k - 1)
                    sum_rows(BLK - 1)
                    dve.wait_ge(oc_ok, BLK * (hg + 1))

            dve.wait_ge(setup_act, 5)
            for b in range(B):
                dve.wait_ge(oT_ps, b + 1)
                dve.scalar_tensor_tensor(out=xs[:, b, :], in0=M[b % 2][:, 0:C], scalar=gt[:, 0:1],
                                         in1=xs[:, b, :], op0=ALU.mult, op1=ALU.add).then_inc(x1_ok, 1)
            dve.memset(run[:], 0.0).then_inc(run_ok, 1)
            dve.memset(sa[:, :, 0:1], 0.0).then_inc(pad_ok, 1)
            dve.memset(sb_[:, :, 0:1], 1.0).then_inc(pad_ok, 1)
            dve.wait_ge(pad_ok, 2)

            def tile_of(b):
                return xs[:, b, :] if isinstance(b, int) else xs[:, bass.ds(b, 1), :].rearrange("p o c -> p (o c)")

            def norm(n, b, ready, count):
                dve.wait_ge(ready, count)
                after(dve.bn_stats(bst[:], tile_of(b)), ln_step, 2 * n + 1)
                after(dve.bn_aggr(mv[:], bst[:]), ln_step, 2 * n + 2)
                dve.tensor_scalar(ve[:], mv[:, 1:2], LN_EPS, None, ALU.add).then_inc(var_ok, 1)
                if not (isinstance(n, int) and n == 0):
                    dve.wait_ge(xT_ps, n)
                dve.wait_ge(rstd_ok, n + 1)
                dve.tensor_scalar(xn[:], tile_of(b), mv[:, 0:1], rs[:, 0:1], ALU.subtract, ALU.mult)\
                    .then_inc(xn_ok, 1)

            def xT_low(n):
                dve.wait_ge(xT_hi_ok, n + 1)
                dve.tensor_tensor(xT_lo[:], xT[:], xT_hi[:].bitcast(F32), ALU.subtract).then_inc(xT_lo_ok, 1)

            def chosen(top, experts, at):
                after(dve.max(v8[:], sc[:, 0:experts]), route, at + 1)
                after(dve.max_index(i8[:], v8[:], sc[:, 0:experts]), route, at + 2)
                after(dve.tensor_copy(f8[:], i8[:]), route, at + 3)
                after(dve.tensor_tensor(eq[:, 0:top, 0:experts],
                                        iota0[:, 0:experts].unsqueeze(1).to_broadcast([P, top, experts]),
                                        f8[:, 0:top].unsqueeze(2).to_broadcast([P, top, experts]),
                                        ALU.is_equal), route, at + 4)
                after(dve.tensor_reduce(mask[:, 0:experts], eq[:, 0:top, 0:experts].rearrange("p k e -> p e k"),
                                        AX.X, ALU.add), route, at + 5)

            def route0(b):
                at = RT0 * b
                dve.wait_ge(exp_ok, b + 1)
                after(dve.tensor_scalar(sc[:], es0[:], 1.0, None, ALU.add), route, at + 1)
                after(dve.reciprocal(sc[:], sc[:]), route, at + 2)
                chosen(TOP0, E0, at + 2)
                dve.tensor_copy(maskb[:], mask[:]).then_inc(mask_ok, 1)

            def weights0(b):
                at = RT0 * b + 7
                dve.tensor_tensor(msc[:], mask[:], sc[:], ALU.mult).then_inc(route, 1)
                dve.tensor_reduce(den[:], v8[:, 0:TOP0], AX.X, ALU.add).then_inc(route, 1)
                dve.wait_ge(route, at + 2)
                after(dve.reciprocal(rden[:], den[:]), route, at + 3)
                dve.wait_ge(pos_ps, b + 1)
                if not (isinstance(b, int) and b == 0):
                    dve.wait_ge(hw_ok, CH0 * b)
                after(dve.scalar_tensor_tensor(out=g[:], in0=PS, scalar=float(CAP0), in1=msc[:],
                                               op0=ALU.is_lt, op1=ALU.mult), route, at + 4)
                dve.tensor_scalar(g[:], g[:], rden[:, 0:1], None, ALU.mult).then_inc(g_ok, 1)
                dve.tensor_tensor(run[:], run[:], maskb[:], ALU.add).then_inc(run_ok, 1)

            def route1(b):
                n = b + B
                at = RT0 * B + RT1 * b
                dve.wait_ge(lg_ps, n + 1)
                dve.tensor_reduce(nmx[:], LG1, AX.X, ALU.max, negate=True).then_inc(nmx_ok, 1)
                dve.wait_ge(exp_ok, n + 1)
                after(dve.tensor_reduce(den[:], es0[:, 0:E1], AX.X, ALU.add), route, at + 1)
                after(dve.reciprocal(rden[:], den[:]), route, at + 2)
                after(dve.tensor_scalar(sc[:, 0:E1], es0[:, 0:E1], rden[:, 0:1], None, ALU.mult), route, at + 3)
                chosen(TOP1, E1, at + 3)
                dve.tensor_tensor(msc[:, 0:E1], mask[:, 0:E1], sc[:, 0:E1], ALU.mult).then_inc(route, 1)
                dve.tensor_reduce(den[:], v8[:, 0:TOP1], AX.X, ALU.add).then_inc(route, 1)
                dve.wait_ge(route, at + 10)
                after(dve.reciprocal(rden[:], den[:]), route, at + 11)
                dve.tensor_scalar(g[:, 0:E1], msc[:, 0:E1], rden[:, 0:1], None, ALU.mult).then_inc(g_ok, 1)

            def act0(b, c):
                dve.wait_ge(sil_ok, NCH * b + c + 1)
                if c > 0:
                    dve.wait_ge(hw_ok, CH0 * b + c)
                if c < CH0:
                    v = U[c % 2][:].rearrange("p n (e w) -> p (n e) w", w=2 * H0)[:, :, H0:2 * H0]
                    dve.tensor_tensor(av[:].rearrange("p (e h) -> p e h", e=CE0),
                                      sil[:].rearrange("p (e h) -> p e h", e=CE0), v, ALU.mult).then_inc(av_ok, 1)
                else:
                    dve.tensor_tensor(av[:, 0:HS0], sil[:, 0:HS0], U[0][:, 0, 0:HS0], ALU.mult).then_inc(av_ok, 1)

            def act1(n, c):
                dve.wait_ge(sil_ok, NCH * n + c + 1)
                if c > 0:
                    dve.wait_ge(hT_ps, NCH * n + c)
                if c < NCH - 1:
                    for e in range(2):
                        a = e * H1
                        ins = dve.scalar_tensor_tensor(out=hw[:, a:a + H1], in0=sil[:, a:a + H1],
                                                       scalar=g[:, 2 * c + e:2 * c + e + 1],
                                                       in1=U[c % 2][:, 1, a:a + H1], op0=ALU.mult, op1=ALU.mult)
                else:
                    ins = dve.tensor_tensor(hw[:, 0:CF1], sil[:, 0:CF1], U[c % 2][:, 1, 0:CF1], ALU.mult)
                ins.then_inc(av_ok, 1)

            def low(n, c, rows, width):
                dve.wait_ge(hT_hi_ok, NCH * n + c + 1)
                dve.tensor_tensor(hT_lo[0:rows, 0:width], HT[0:rows, 0:width],
                                  hT_hi[0:rows, 0:width].bitcast(F32), ALU.subtract).then_inc(hT_lo_ok, 1)

            def low0(b, c):
                low(b, c, P if c < CH0 else HS0, CF0 if c < CH0 else P)

            def add(n, b, gate, done):
                dve.wait_ge(down_ps, NCH * (n + 1))
                dve.scalar_tensor_tensor(out=tile_of(b), in0=DN[:, 0:C], scalar=gt[:, gate:gate + 1],
                                         in1=tile_of(b), op0=ALU.mult, op1=ALU.add).then_inc(done, 1)

            def norm2(b):
                dve.wait_ge(x2_ok, b + 1)
                after(dve.bn_stats(bst2[:], tile_of(b)), ln2_step, 2 * b + 1)
                after(dve.bn_aggr(mv2[:], bst2[:]), ln2_step, 2 * b + 2)
                dve.tensor_scalar(ve2[:], mv2[:, 1:2], LN_EPS, None, ALU.add).then_inc(var2_ok, 1)
                dve.wait_ge(rstd2_ok, b + 1)
                dve.tensor_scalar(xn2[:], tile_of(b), mv2[:, 0:1], rs2[:, 0:1], ALU.subtract, ALU.mult)\
                    .then_inc(xn2_ok, 1)

            def scan(b):
                at = WK * b
                v = ct[:, :, b, :] if isinstance(b, int) else \
                    ct[:, :, bass.ds(b, 1), :].rearrange("p t o r -> p t (o r)")
                dve.wait_ge(ct_in, 16)
                dve.wait_ge(ek_ok, b + 1)
                after(dve.tensor_tensor(ev[:], ek[:], v, ALU.mult), wk_step, at + 1)
                for t in range(NT):
                    for dst, src in ((sa, ev), (sb_, ek)):
                        dve.tensor_tensor_scan(dst[:, t, 1:R + 1], dc[:, t:t + 1].to_broadcast([P, R]),
                                               src[:, t, :], 0.0, ALU.mult, ALU.add).then_inc(wk_step, 1)

            def quotient(b):
                at = WK * b + 5
                v = ct[:, :, b, :] if isinstance(b, int) else \
                    ct[:, :, bass.ds(b, 1), :].rearrange("p t o r -> p t (o r)")
                dve.wait_ge(wk_step, at)
                for t in range(NT):
                    for s in (sa, sb_):
                        dve.tensor_scalar(s[:, t, 0:R], s[:, t, 0:R], c1[:, t:t + 1], None, ALU.mult)\
                            .then_inc(wk_step, 1)
                dve.wait_ge(wk_step, at + 4)
                for t in range(NT):
                    for own, s in ((ek, sb_), (ev, sa)):
                        dve.scalar_tensor_tensor(out=own[:, t, :], in0=own[:, t, :], scalar=c2[:, t:t + 1],
                                                 in1=s[:, t, 0:R], op0=ALU.mult, op1=ALU.add).then_inc(wk_step, 1)
                dve.wait_ge(wk_step, at + 8)
                after(dve.reciprocal(ek[:], ek[:]), wk_step, at + 9)
                after(dve.tensor_tensor(yt, ev[:], ek[:], ALU.mult), wk_step, at + 10)
                dve.tensor_copy(yt[:, :, 0:1], v[:, :, 0:1]).then_inc(y_ok, 1)

            def add_y(b):
                dve.wait_ge(yT_ps, b + 1)
                dve.scalar_tensor_tensor(out=tile_of(b), in0=M1[:, 0:C], scalar=gt[:, 1:2],
                                         in1=tile_of(b), op0=ALU.mult, op1=ALU.add).then_inc(x3_ok, 1)

            def tile0(b, first, last):
                if not first:
                    norm2(b - 1)
                act0(b, 0)
                act0(b, 1)
                low0(b, 0)
                if not first:
                    scan(b - 1)
                act0(b, 2)
                low0(b, 1)
                if not first:
                    quotient(b - 1)
                act0(b, 3)
                low0(b, 2)
                if not first:
                    add_y(b - 1)
                act0(b, 4)
                if last:
                    norm(B, 0, x3_ok, 1)
                else:
                    norm(b + 1, b + 1, x1_ok, B)
                low0(b, 3)
                xT_low(b + 1)
                if not last:
                    route0(b + 1)
                else:
                    route1(0)
                low0(b, 4)
                if not last:
                    weights0(b + 1)
                add(b, b, 2, x2_ok)

            norm(0, 0, x1_ok, B)
            xT_low(0)
            route0(0)
            weights0(0)
            tile0(0, True, False)
            with dve.Fori(1, B - 1) as b:
                tile0(b, False, False)
            tile0(B - 1, False, True)
            norm2(B - 1)
            dve.memset(hw[:, CF1:CP1], 0.0).then_inc(pad_ok, 1)
            dve.wait_ge(pad_ok, 3)

            def tile1(b, first, last):
                n = b + B
                act1(n, 0)
                if first:
                    scan(B - 1)
                for c in range(1, NCH):
                    act1(n, c)
                    if first and c == 1:
                        quotient(B - 1)
                        add_y(B - 1)
                    low(n, c - 1, P, CP1)
                if not last:
                    norm(n + 1, b + 1, x3_ok, b + 2)
                    xT_low(n + 1)
                    route1(b + 1)
                low(n, NCH - 1, P, CP1)
                add(n, b, 3, x4_ok)

            tile1(0, True, False)
            with dve.Fori(1, B - 1) as b:
                tile1(b, False, False)
            tile1(B - 1, False, True)


_SHAPE = (B, R, C)


def kernel(x, ctx_2048, g_xattn, g_ffn, L0_xattn_ssm_kernel, L0_xattn_D, L0_ffn_w_gate, L0_ffn_w_shared_up,
           L0_ffn_w_shared_down, L0_ffn_w_up, L0_ffn_w_down, L1_xattn_time_decay, L1_xattn_time_first,
           L1_ffn_gate_weight, L1_ffn_w_gate, L1_ffn_w_up, L1_ffn_w_down, L1_ffn_w_shared_gate,
           L1_ffn_w_shared_up, L1_ffn_w_shared_down):
    import numpy as np
    import concourse.bacc as bacc
    from concourse.bass_utils import run_bass_kernel_spmd as run

    f32 = np.float32

    def channels_first(a):
        return a.reshape(NT, P, -1).transpose(1, 0, 2).reshape(P, -1)

    def rows_first(a):
        return a.reshape(-1, P, C).transpose(1, 0, 2).reshape(P, -1)

    x = np.asarray(x)
    ctx = np.asarray(ctx_2048).transpose(2, 0, 1).reshape(NT, P, B, R)
    ctx_t = ctx.transpose(1, 0, 2, 3)
    ctx_rev = ctx[:, ::-1].transpose(1, 0, 2, 3)
    taps = np.asarray(L0_xattn_ssm_kernel)
    conv_pad = np.concatenate([np.zeros((HEADS, P - 1), f32), taps, np.zeros((HEADS, 1), f32)], axis=1)

    up0 = np.asarray(L0_ffn_w_up).transpose(1, 0, 2).reshape(C, -1)
    up0 = channels_first(np.concatenate([up0, np.asarray(L0_ffn_w_shared_up)], axis=1))
    down0 = np.concatenate([np.asarray(L0_ffn_w_down).reshape(-1, C), np.asarray(L0_ffn_w_shared_down),
                            np.zeros((P - HS0, C), f32)])
    w0 = np.concatenate([up0, rows_first(down0)], axis=1)

    def cols(w, shared):
        return np.concatenate([np.asarray(w).reshape(-1, C), np.asarray(shared)]).T.reshape(C, NCH, CF1)

    up1 = np.stack([cols(L1_ffn_w_gate, L1_ffn_w_shared_gate), cols(L1_ffn_w_up, L1_ffn_w_shared_up)], axis=2)
    up1 = channels_first(up1.reshape(C, -1))
    down1 = np.concatenate([np.asarray(L1_ffn_w_down).transpose(0, 2, 1).reshape(-1, C),
                            np.asarray(L1_ffn_w_shared_down).T]).reshape(NCH, CF1, C)
    down1 = np.concatenate([down1, np.zeros((NCH, CP1 - CF1, C), f32)], axis=1).reshape(-1, C)
    w1 = np.concatenate([up1, rows_first(down1)], axis=1)

    arrays = {
        "x": x,
        "ctx_t": ctx_t,
        "ctx_rev": ctx_rev,
        "conv_pad": conv_pad,
        "conv_d": np.asarray(L0_xattn_D).reshape(1, HEADS),
        "gates": np.concatenate([np.asarray(g_xattn), np.asarray(g_ffn)]).reshape(1, 4),
        "w0": w0,
        "w_gate0": channels_first(np.asarray(L0_ffn_w_gate)).reshape(P, NT, E0),
        "w1": w1,
        "w_gate1": channels_first(np.asarray(L1_ffn_gate_weight).T).reshape(P, NT, E1),
        "decay": np.asarray(L1_xattn_time_decay).reshape(NT, P).T,
        "first": np.asarray(L1_xattn_time_first).reshape(NT, P).T,
    }
    arrays = {f"in_{k}": np.ascontiguousarray(v) for k, v in arrays.items()}
    nc = bacc.Bacc("TRN2", target_bir_lowering=False, num_devices=1)
    args = [nc.dram_tensor(k, v.shape, F32, kind="ExternalInput").ap() for k, v in arrays.items()]
    args.append(nc.dram_tensor("out_x", _SHAPE, F32, kind="ExternalOutput").ap())
    build(nc, *args)
    r = run(nc, [arrays], core_ids=[0])
    return r.results[0]["out_x"]
```

```python
from contextlib import ExitStack

import concourse.bass as bass
from concourse import mybir

F32 = mybir.dt.float32
F32R = mybir.dt.float32r
BF16 = mybir.dt.bfloat16
U32 = mybir.dt.uint32
I32 = mybir.dt.int32
ALU = mybir.AluOpType
ACT = mybir.ActivationFunctionType
AX = mybir.AxisListType

P = 128
B, R, C = 8, 128, 256
NT = C // P
HEADS, HD = 16, 8
HG = 4
NHG = HEADS // HG
KW = HD * HD
BLK = NT * HG
LN_EPS = 1e-5

CF = 352
KT = (CF + P - 1) // P
CP = KT * P

E0, H0, TOP0, CAP0, HS0 = 64, 32, 6, 128, 64
ES0 = E0 + HS0 // H0
CH0 = ES0 * H0 // CF
CE0 = CF // H0
UW0 = CH0 * 2 * CF
NK0 = CH0 * KT

E1, H1, TOP1, HS1 = 8, 176, 2, 352
CH1 = (E1 * H1 + HS1) // CF
UW1 = CH1 * 2 * CF
NK1 = CH1 * KT
Q1 = CH0 * B

SL = 4
PC0 = (NT * UW0 + NK0 * C) // (NHG * SL)
NU1 = 2 * B
PCU1 = NT * UW1 // NU1
ND1 = 2 * SL
PCD1 = NK1 * C // ND1

RT0, RT1 = 11, 11
WK = 10
PK = 4
Y0 = 4

S_D, S_GATE, S_TD, S_FS = 0, HEADS, HEADS + 4, HEADS + 4 + NT
S_WG0 = S_FS + NT
S_WG1 = S_WG0 + NT * E0
SMALL = S_WG1 + NT * E1


def build(nc, small_d, x, ctx_t, ctx_rev, conv_pad, w0, w1, out):
    es = ExitStack()
    with es:
        def sb(name, shape, dt=F32, stack=es):
            return stack.enter_context(nc.sbuf_tensor(name, shape, dt))

        def pb(name, shape):
            return es.enter_context(nc.psum_tensor(name, shape, F32))

        def sem(name):
            return es.enter_context(nc.semaphore(name))

        small = sb("small", [P, SMALL])
        db = small[:, S_D:S_D + HEADS]
        gates_sb = small[:, S_GATE:S_GATE + 4]
        td = small[:, S_TD:S_TD + NT]
        fs = small[:, S_FS:S_FS + NT]
        wg0 = small[:, S_WG0:S_WG1].rearrange("p (t e) -> p t e", t=NT)
        wg1 = small[:, S_WG1:SMALL].rearrange("p (t e) -> p t e", t=NT)
        xs = sb("xs", [P, B, C])
        w0_hi = sb("w0_hi", [P, NT * UW0 + NK0 * C], F32R)
        w0_lo = sb("w0_lo", [P, NT * UW0 + NK0 * C], F32R)
        stage1 = sb("stage1", [P, SL, max(PCU1, PCD1)])
        ident = sb("ident", [P, P])
        tri = sb("tri", [P, P], BF16)
        ones = sb("ones", [P, P], BF16)
        iota0 = sb("iota0", [P, E0])
        nhalf = sb("nhalf", [P, B])
        gt = sb("gt", [P, 4])
        tdc = sb("tdc", [P, NT])
        etd = sb("etd", [P, NT])
        dc = sb("dc", [P, NT])
        umax = sb("umax", [P, NT])
        umin = sb("umin", [P, NT])
        c1 = sb("c1", [P, NT])
        c2 = sb("c2", [P, NT])
        bst = sb("bst", [P, 6])
        mv = sb("mv", [P, 2])
        ve = sb("ve", [P, 1])
        rs = sb("rs", [P, 1])
        xn = sb("xn", [P, C])

        a_stage = ExitStack()
        anti = sb("anti", [P, P], stack=a_stage)
        bstq = sb("bstq", [P, B, 6], stack=a_stage)
        mvq = sb("mvq", [P, B, 2], stack=a_stage)
        veq = sb("veq", [P, B], stack=a_stage)
        rsq = sb("rsq", [P, B], stack=a_stage)
        iota_i = sb("iota_i", [P, E0], I32, stack=a_stage)
        tz = sb("tz", [P, 2, HG, 2 * P], stack=a_stage)
        z = sb("z", [P, NT, HG, B * KW], stack=a_stage)
        qt = sb("qt", [P, NT, B, R], stack=a_stage)
        prod = sb("prod", [P, 4, B * KW], stack=a_stage)
        oc = sb("oc", [P, NT, B, R], stack=a_stage)
        cr = sb("cr", [P, NT, B, R], stack=a_stage)
        qn = oc[:].rearrange("p t b r -> p (t b r)").rearrange("p (b c) -> p b c", b=B)
        stage0 = sb("stage0", [P, SL, PC0], stack=a_stage)
        a_stage.close()

        w1u_hi = sb("w1u_hi", [P, NT * UW1], F32R)
        w1u_lo = sb("w1u_lo", [P, NT * UW1], F32R)
        ct = sb("ct", [P, NT, B, R])
        sil = sb("sil", [P, CF])
        av = sb("av", [P, CF])
        hw = sb("hw", [P, 2, CP])
        hT_hi = sb("hT_hi", [P, CP], F32R)
        hT_lo = sb("hT_lo", [P, CP], F32R)
        ek = sb("ek", [P, NT, R])
        ev = sb("ev", [P, NT, R])
        sa = sb("sa", [P, NT, R + 1])
        sb_ = sb("sb_", [P, NT, R + 1])
        xn2 = sb("xn2", [P, C])
        yt = xn2[:, :].rearrange("p (t r) -> p t r", t=NT)
        eq = sb("eq", [P, TOP0, E0])
        xT = sb("xT", [P, 2, NT, R])
        xT_hi = sb("xT_hi", [P, 2, NT, R], F32R)
        xT_lo = sb("xT_lo", [P, 2, NT, R], F32R)
        es0 = sb("es0", [P, E0])
        sc = sb("sc", [P, E0])
        v8 = sb("v8", [P, 8])
        i8 = sb("i8", [P, 8], U32)
        f8 = sb("f8", [P, 8])
        mask = sb("mask", [P, E0])
        maskb = sb("maskb", [P, E0], BF16)
        run = sb("run", [P, E0], BF16)
        den = sb("den", [P, 1])
        rden = sb("rden", [P, 1])
        msc = sb("msc", [P, E0])
        g = sb("g", [P, 2, ES0])
        nmx = sb("nmx", [P, 1])
        bst2 = sb("bst2", [P, 6])
        mv2 = sb("mv2", [P, 2])
        ve2 = sb("ve2", [P, 1])
        rs2 = sb("rs2", [P, 1])

        U = [pb(f"U{i}", [P, 2, 512]) for i in range(2)]
        HT = pb("HT", [P, 512])
        DN = pb("DN", [P, 512])
        M0 = pb("M0", [P, 512])
        M1 = pb("M1", [P, 512])
        Y = [U[0][:, 0, :], U[0][:, 1, :], U[1][:, 0, :], U[1][:, 1, :]]
        M = [M0, M1, HT, DN]
        XT, LG, PS = M0[:, 0:C], M0[:, C:C + E0], M0[:, C + E0:C + 2 * E0]
        LG1 = M0[:, C:C + E1]

        def up0(low, t, a, b):
            return (w0_hi, w0_lo)[low][:, t * UW0 + a:t * UW0 + b]

        def up1(low, t, a, b):
            return (w1u_hi, w1u_lo)[low][:, t * UW1 + a:t * UW1 + b]

        def down0(low, k):
            return (w0_hi, w0_lo)[low][:, NT * UW0 + k * C:NT * UW0 + (k + 1) * C]

        D1_AT = NK1 * C

        def down1(low, k):
            return w0_hi[:, low * D1_AT + k * C:low * D1_AT + (k + 1) * C]

        ctx_in = [sem(f"ctx_in{i}") for i in range(NT)]
        x_in, small_in, ct_in, out_done = sem("x_in"), sem("small_in"), sem("ct_in"), sem("out_done")
        toep0_in, toep_in = sem("toep0_in"), sem("toep_in")
        stage0_in = [sem(f"stage0_in{i}") for i in range(SL)]
        stage1_in = [sem(f"stage1_in{i}") for i in range(SL)]
        memset_ok, const_ok, iota_ok = sem("memset_ok"), sem("const_ok"), sem("iota_ok")
        passed_dve = sem("passed_dve")
        setup_dve, setup_act = sem("setup_dve"), sem("setup_act")
        s0_hi, s0_lo = sem("s0_hi"), sem("s0_lo")
        s1_hi, s1_lo = sem("s1_hi"), sem("s1_lo")
        qstep, qvar_ok, qrstd_ok, qn_ok = sem("qstep"), sem("qvar_ok"), sem("qrstd_ok"), sem("qn_ok")
        qT_ps, qT_ok = sem("qT_ps"), sem("qT_ok")
        toep_ok, z_dve, z_pool = sem("toep_ok"), sem("z_dve"), sem("z_pool")
        conv_ps, oc_ok = sem("conv_ps"), sem("oc_ok")
        prod_ok = sem("prod_ok")
        oT_ps, x1_ok = sem("oT_ps"), sem("x1_ok")
        ln_step, var_ok, rstd_ok, xn_ok = sem("ln_step"), sem("var_ok"), sem("rstd_ok"), sem("xn_ok")
        xT_ps, xT_ok, xT_hi_ok, xT_lo_ok = sem("xT_ps"), sem("xT_ok"), sem("xT_hi_ok"), sem("xT_lo_ok")
        lg_ps, nmx_ok, exp_ok, route, mask_ok = sem("lg_ps"), sem("nmx_ok"), sem("exp_ok"), sem("route"), sem("mask_ok")
        pos_ps, g_ok, run_ok = sem("pos_ps"), sem("g_ok"), sem("run_ok")
        up_ps, sil_ok, av_ok, hw_ok = sem("up_ps"), sem("sil_ok"), sem("av_ok"), sem("hw_ok")
        hT_ps, hT_hi_ok, hT_lo_ok, down_ps = sem("hT_ps"), sem("hT_hi_ok"), sem("hT_lo_ok"), sem("down_ps")
        x2_ok, x4_ok, pad_ok, hpad_ok = sem("x2_ok"), sem("x4_ok"), sem("pad_ok"), sem("hpad_ok")
        ln2_step, var2_ok, rstd2_ok, xn2_ok = sem("ln2_step"), sem("var2_ok"), sem("rstd2_ok"), sem("xn2_ok")
        kT_ps, ek_ok, ev_ok, wk, pk = sem("kT_ps"), sem("ek_ok"), sem("ev_ok"), sem("wk"), sem("pk")
        y_ok, yT_ps, x3_ok = sem("y_ok"), sem("yT_ps"), sem("x3_ok")

        block = es.enter_context(nc.Block())

        def dyn(t, b):
            if isinstance(b, int):
                return t[:, b]
            return t[:, bass.ds(b, 1)].rearrange("p o c -> p (o c)")

        def ctx_of(b):
            if isinstance(b, int):
                return ct[:, :, b, :]
            return ct[:, :, bass.ds(b, 1), :].rearrange("p t o r -> p t (o r)")

        @block.sync
        def _(sp):
            def toeplitz(hg, signal):
                src = bass.AP(conv_pad.tensor, hg * (HG * 3 * P), [[1, P], [3 * P, HG], [1, 2 * P]])
                sp.dma_start(tz[:, hg % 2], src).then_inc(signal, 16)

            def pieces0(grp):
                for k in range(SL):
                    if grp > 0:
                        sp.wait_ge(s0_lo, SL * (grp - 1) + k + 1)
                    at = (grp * SL + k) * PC0
                    sp.dma_start(stage0[:, k, :], w0[:, at:at + PC0]).then_inc(stage0_in[k], 16)

            sp.dma_start(small[:], small_d).then_inc(small_in, 16)
            sp.dma_start(cr[:, 0], ctx_rev[:, 0]).then_inc(ctx_in[0], 16)
            toeplitz(0, toep0_in)
            sp.dma_start(cr[:, 1], ctx_rev[:, 1]).then_inc(ctx_in[1], 16)
            sp.dma_start(xs[:], x.rearrange("b r c -> r b c")).then_inc(x_in, 16)
            toeplitz(1, toep_in)
            pieces0(0)
            for hg in range(2, NHG):
                pieces0(hg - 1)
                sp.wait_ge(toep_in, 16 * (hg - 1))
                sp.wait_ge(conv_ps, BLK * (hg - 1))
                toeplitz(hg, toep_in)
            pieces0(NHG - 1)
            sp.wait_ge(x1_ok, B)
            sp.wait_ge(s0_lo, NHG * SL)

            def piece1(m, k, at, width):
                sp.dma_start(stage1[:, k, 0:width], w1[:, bass.ds(at, width)]).then_inc(stage1_in[k], 16)

            for k in range(SL):
                piece1(k, k, k * PCU1, PCU1)
            sp.dma_start(ct[:], ctx_t).then_inc(ct_in, 16)
            with sp.Fori(1, NU1 // SL) as i:
                for k in range(SL):
                    sp.wait_ge(s1_lo, SL * i + (k + 1 - SL))
                    piece1(k, k, (SL * i + k) * PCU1, PCU1)
            with sp.Fori(NU1 // SL, (NU1 + ND1) // SL) as i:
                for k in range(SL):
                    sp.wait_ge(s1_lo, SL * i + (k + 1 - SL))
                    piece1(k, k, (SL * i + k) * PCD1 + (NT * UW1 - NU1 * PCD1), PCD1)
            with sp.Fori(0, B) as b:
                sp.wait_ge(x4_ok, b + 1)
                sp.dma_start(out[bass.ds(b, 1)].rearrange("b r c -> r (b c)"), dyn(xs, b)).then_inc(out_done, 16)
            sp.wait_ge(out_done, 16 * B)

        @block.gpsimd
        def _(pool):
            pool.memset(ident[:], 0.0).then_inc(memset_ok, 1)
            pool.memset(anti[:], 0.0).then_inc(memset_ok, 1)
            pool.memset(tri[:], 1.0).then_inc(memset_ok, 1)
            pool.memset(ones[:], 1.0).then_inc(const_ok, 1)
            pool.memset(nhalf[:], -0.5).then_inc(const_ok, 1)
            pool.iota(iota_i[:], [[1, E0]], base=0, channel_multiplier=0).then_inc(iota_ok, 1)
            pool.wait_ge(memset_ok, 3)
            pool.affine_select(out=ident[:], in_=ident[:], compare_op=ALU.not_equal, fill=1.0, base=0,
                               pattern=[[-1, P]], channel_multiplier=1).then_inc(const_ok, 1)
            pool.affine_select(out=anti[:], in_=anti[:], compare_op=ALU.not_equal, fill=1.0, base=-(P - 1),
                               pattern=[[1, P]], channel_multiplier=1).then_inc(const_ok, 1)
            pool.affine_select(out=tri[:], in_=tri[:], compare_op=ALU.is_gt, fill=0.0, base=0,
                               pattern=[[1, P]], channel_multiplier=-1).then_inc(const_ok, 1)
            pool.wait_ge(const_ok, 5)

            def z_of(hg, h):
                rows = cr[:, 1, :, bass.ds(hg * (HG * HD) + h * HD, HD)]
                pool.tensor_tensor(z[:, 1, h, :].rearrange("p (b i j) -> p b i j", b=B, i=HD),
                                   rows.unsqueeze(3).to_broadcast([P, B, HD, HD]),
                                   rows.unsqueeze(2).to_broadcast([P, B, HD, HD]), ALU.mult).then_inc(z_pool, 1)

            def low0(m, k):
                pool.wait_ge(s0_hi, m + 1)
                at = bass.ds(m * PC0, PC0)
                pool.tensor_tensor(w0_lo[:, at], stage0[:, k, :], w0_hi[:, at].bitcast(F32),
                                   ALU.subtract).then_inc(s0_lo, 1)

            pool.wait_ge(ctx_in[1], 16)
            z_of(0, 0)
            z_of(0, 1)
            pool.wait_ge(qvar_ok, 1)
            pool.tensor_tensor(rsq[:], veq[:], nhalf[:], ALU.pow).then_inc(qrstd_ok, 1)
            z_of(0, 2)
            z_of(0, 3)
            with pool.Fori(0, NHG - 1) as hg:
                for h in range(HG):
                    low0(SL * hg + h, h)
                    pool.wait_ge(conv_ps, BLK * hg + NT * (h + 1))
                    z_of(hg + 1, h)
            for k in range(SL):
                low0(SL * (NHG - 1) + k, k)

            def rstd(n):
                pool.wait_ge(var_ok, n + 1)
                pool.tensor_tensor(rs[:], ve[:], nhalf[:, 0:1], ALU.pow).then_inc(rstd_ok, 1)

            def rstd2(b):
                pool.wait_ge(var2_ok, b + 1)
                pool.tensor_tensor(rs2[:], ve2[:], nhalf[:, 0:1], ALU.pow).then_inc(rstd2_ok, 1)

            def xT_low(n, par):
                pool.wait_ge(xT_hi_ok, n + 1)
                pool.tensor_tensor(xT_lo[:, par], xT[:, par], xT_hi[:, par].bitcast(F32), ALU.subtract)\
                    .then_inc(xT_lo_ok, 1)

            def weigh(b, c, par):
                q = CH0 * b + c
                pool.wait_ge(av_ok, q + 1)
                if c >= 2 or not (isinstance(b, int) and b == 0):
                    pool.wait_ge(hT_ps, q - 1)
                grp = g[:, par, c * CE0:(c + 1) * CE0].unsqueeze(2).to_broadcast([P, CE0, H0])
                pool.tensor_tensor(hw[:, c % 2, 0:CF].rearrange("p (e h) -> p e h", e=CE0),
                                   av[:].rearrange("p (e h) -> p e h", e=CE0), grp, ALU.mult)\
                    .then_inc(hw_ok, 1)

            def low_up1(m, k):
                pool.wait_ge(s1_hi, m + 1)
                at = bass.ds(m * PCU1, PCU1)
                pool.tensor_tensor(w1u_lo[:, at], stage1[:, k, 0:PCU1], w1u_hi[:, at].bitcast(F32),
                                   ALU.subtract).then_inc(s1_lo, 1)

            def own_terms(b):
                pool.wait_ge(ct_in, 16)
                pool.wait_ge(ek_ok, b + 1)
                pool.tensor_tensor(ev[:], ek[:], ctx_of(b), ALU.mult).then_inc(ev_ok, 1)

            def scaled_sums(b):
                pool.wait_ge(wk, WK * b + 4)
                for s in (sb_, sa):
                    pool.tensor_tensor(s[:, :, 0:R], s[:, :, 0:R], c1[:].unsqueeze(2).to_broadcast([P, NT, R]),
                                       ALU.mult).then_inc(pk, 1)

            def divided(b):
                pool.wait_ge(wk, WK * b + WK)
                pool.tensor_tensor(yt, ev[:], ek[:], ALU.mult).then_inc(pk, 1)
                pool.wait_ge(pk, PK * b + 3)
                pool.sem_inc(pk, 1)
                pool.tensor_copy(yt[:, :, 0:1], ctx_of(b)[:, :, 0:1]).then_inc(y_ok, 1)

            def tile0(b, par, first):
                pool.wait_ge(g_ok, b + 1)
                weigh(b, 0, par)
                rstd(b + 1)
                weigh(b, 1, par)
                if not first:
                    rstd2(b - 1)
                xT_low(b + 1, 1 - par)
                weigh(b, 2, par)
                low_up1(2 * b, 2 * par)
                weigh(b, 3, par)
                if not first:
                    own_terms(b - 1)
                weigh(b, 4, par)
                if not first:
                    scaled_sums(b - 1)
                low_up1(2 * b + 1, 2 * par + 1)
                weigh(b, 5, par)
                if not first:
                    divided(b - 1)

            rstd(0)
            xT_low(0, 0)
            tile0(0, 0, True)
            with pool.Fori(0, (B - 2) // 2) as i:
                for k in range(2):
                    tile0(2 * i + (k + 1), 1 - k, False)
            tile0(B - 1, 1, False)

            def low_down1(k):
                pool.wait_ge(s1_hi, NU1 + k + 1)
                at = k * PCD1
                pool.tensor_tensor(w0_hi[:, D1_AT + at:D1_AT + at + PCD1], stage1[:, k % SL, 0:PCD1],
                                   w0_hi[:, at:at + PCD1].bitcast(F32), ALU.subtract).then_inc(s1_lo, 1)

            for k in range(4):
                low_down1(k)
            rstd(B + 1)
            for k in range(4, ND1):
                low_down1(k)
            rstd2(B - 1)
            xT_low(B + 1, 1)
            own_terms(B - 1)
            scaled_sums(B - 1)
            divided(B - 1)
            with pool.Fori(0, (B - 2) // 2) as i:
                for k in range(2):
                    n = 2 * i + (k + 2 + B)
                    rstd(n)
                    xT_low(n, k)

        @block.scalar
        def _(act):
            act.wait_ge(small_in, 16)
            act.activation(gt[:], gates_sb, ACT.Tanh).then_inc(setup_act, 1)
            act.wait_ge(setup_dve, 4)
            act.activation(etd[:], tdc[:], ACT.Exp).then_inc(setup_act, 1)
            act.wait_ge(setup_act, 2)
            act.activation(dc[:], etd[:], ACT.Exp, scale=-1.0).then_inc(setup_act, 1)
            act.activation(c1[:], umax[:], ACT.Exp, scale=-1.0).then_inc(setup_act, 1)
            act.activation(c2[:], umin[:], ACT.Exp).then_inc(setup_act, 1)
            for b in range(B):
                act.wait_ge(qT_ps, b + 1)
                act.activation(qt[:, :, b, :], M[b % 4][:, 0:C].rearrange("p (t r) -> p t r", t=NT),
                               ACT.Copy).then_inc(qT_ok, 1)
            with act.Fori(0, NHG) as grp:
                for k in range(SL):
                    act.wait_ge(stage0_in[k], 16 * (grp + 1))
                    act.activation(w0_hi[:, bass.ds((grp * SL + k) * PC0, PC0)], stage0[:, k, :],
                                   ACT.Copy).then_inc(s0_hi, 1)

            def turned(n, par):
                act.wait_ge(xT_ps, n + 1)
                act.activation(xT[:, par].rearrange("p t r -> p (t r)"), XT, ACT.Copy).then_inc(xT_ok, 1)
                act.wait_ge(xT_ok, n + 1)
                act.activation(xT_hi[:, par], xT[:, par], ACT.Copy).then_inc(xT_hi_ok, 1)

            def exp0(b):
                act.wait_ge(lg_ps, b + 1)
                act.activation(es0[:], LG, ACT.Exp, scale=-1.0).then_inc(exp_ok, 1)

            def exp1(b):
                act.wait_ge(nmx_ok, b + 1)
                act.activation(es0[:, 0:E1], LG1, ACT.Exp, bias=nmx[:, 0:1]).then_inc(exp_ok, 1)

            def ek_of(b):
                act.wait_ge(kT_ps, b + 1)
                act.activation(ek[:].rearrange("p t r -> p (t r)"), M1[:, 0:C], ACT.Exp).then_inc(ek_ok, 1)

            def silu(q, par, read):
                act.wait_ge(up_ps, q + 1)
                if not (isinstance(q, int) and q == 0):
                    act.wait_ge(read, q)
                act.activation(sil[:], U[par][:, 0, 0:CF], ACT.Silu).then_inc(sil_ok, 1)

            def high(q):
                act.wait_ge(hT_ps, q + 1)
                if not (isinstance(q, int) and q == 0):
                    act.wait_ge(down_ps, q)
                act.activation(hT_hi[:], HT[:, 0:CP], ACT.Copy).then_inc(hT_hi_ok, 1)

            def split_piece(b, j, k, loads):
                act.wait_ge(stage1_in[k], 16 * loads)
                act.activation(w1u_hi[:, bass.ds((2 * b + j) * PCU1, PCU1)], stage1[:, k, 0:PCU1], ACT.Copy)\
                    .then_inc(s1_hi, 1)

            def tile0(b, par, first, last, loads):
                for c in range(CH0):
                    q = CH0 * b + c
                    silu(q, c % 2, av_ok)
                    if not (first and c == 0):
                        high(q - 1)
                    if c == 0:
                        split_piece(b, 0, 2 * par, loads)
                    if c == 1:
                        turned(b + 1, 1 - par)
                    if c == 2:
                        if last:
                            exp1(0)
                        else:
                            exp0(b + 1)
                        if not first:
                            ek_of(b - 1)
                    if c == 4:
                        split_piece(b, 1, 2 * par + 1, loads)

            turned(0, 0)
            exp0(0)
            tile0(0, 0, True, False, 1)
            with act.Fori(0, (B - 2) // 2) as i:
                for k in range(2):
                    tile0(2 * i + (k + 1), 1 - k, False, False, i + (k + 1))
            tile0(B - 1, 1, False, True, B // 2)

            def split_down1(k):
                act.wait_ge(stage1_in[k % SL], 16 * (NU1 // SL + k // SL + 1))
                act.activation(w0_hi[:, k * PCD1:(k + 1) * PCD1], stage1[:, k % SL, 0:PCD1], ACT.Copy)\
                    .then_inc(s1_hi, 1)

            def tile1(b, par, first, last):
                for c in range(CH1):
                    q = CH1 * b + (Q1 + c)
                    silu(q, (CH1 * par + c) % 2, av_ok if first and c == 0 else hw_ok)
                    high(q - 1)
                    if first and c < 2:
                        for k in range(4 * c, 4 * c + 4):
                            split_down1(k)
                    if c == 1 and not last:
                        turned(b + (B + 1), 1 - par)
                    if c == 2:
                        if not last:
                            exp1(b + 1)
                        if first:
                            ek_of(B - 1)
                if last:
                    high(q)

            tile1(0, 0, True, False)
            with act.Fori(0, (B - 2) // 2) as i:
                for k in range(2):
                    tile1(2 * i + (k + 1), 1 - k, False, False)
            tile1(B - 1, 1, False, True)

        @block.tensor
        def _(pe):
            def turn(dst, src):
                return pe.transpose(dst, src, ident[:])

            pe.wait_ge(const_ok, 5)

            def q_turn(b):
                pe.wait_ge(qn_ok, b + 1)
                if b >= 4:
                    pe.wait_ge(qT_ok, b - 3)
                for t in range(NT):
                    mm = turn(M[b % 4][:, t * P:(t + 1) * P], qn[:, b, t * P:(t + 1) * P])
                mm.then_inc(qT_ps, 1)

            for b in range(B):
                q_turn(b)
            with pe.Fori(0, NHG // 2) as i:
                for par in range(2):
                    hg = 2 * i + par
                    for h in range(HG):
                        k = NT * h
                        pe.wait_ge(toep_ok, HG * hg + h + 1)
                        pe.wait_ge(z_dve, HG * hg + h + 1)
                        pe.wait_ge(prod_ok, BLK * hg + k + 1)
                        pe.matmul(Y[k % Y0], tz[:, par, h, 0:P], z[:, 0, h, :], start=True, stop=True)\
                            .then_inc(conv_ps, 1)
                        pe.wait_ge(z_pool, HG * hg + h + 1)
                        pe.wait_ge(prod_ok, BLK * hg + k + 2)
                        pe.matmul(Y[(k + 1) % Y0], tz[:, par, h, P:2 * P], z[:, 0, h, :], start=True, stop=False)
                        pe.matmul(Y[(k + 1) % Y0], tz[:, par, h, 0:P], z[:, 1, h, :], start=False, stop=True)\
                            .then_inc(conv_ps, 1)

            pe.wait_ge(oc_ok, BLK * NHG)

            def o_turn(b):
                if b >= 4:
                    pe.wait_ge(x1_ok, b - 3)
                for t in range(NT):
                    mm = turn(M[b % 4][:, t * P:(t + 1) * P], oc[:, t, b, :])
                mm.then_inc(oT_ps, 1)

            for b in range(B):
                o_turn(b)

            def pre(n):
                pe.wait_ge(xn_ok, n + 1)
                if isinstance(n, int) and n == 0:
                    pe.wait_ge(x1_ok, B)
                else:
                    pe.wait_ge(g_ok, n)
                for t in range(NT):
                    mm = turn(XT[:, t * P:(t + 1) * P], xn[:, t * P:(t + 1) * P])
                mm.then_inc(xT_ps, 1)

            def logits(n, par, w, dst):
                pe.wait_ge(xT_ok, n + 1)
                for t in range(NT):
                    mm = pe.matmul(dst, xT[:, par, t, :], w[:, t, :], start=(t == 0), stop=(t == NT - 1))
                mm.then_inc(lg_ps, 1)

            def places(b):
                pe.wait_ge(mask_ok, b + 1)
                pe.wait_ge(run_ok, b + 1)
                pe.matmul(PS, tri[:], maskb[:], start=True, stop=False)
                pe.matmul(PS, ones[:], run[:], start=False, stop=True).then_inc(pos_ps, 1)

            def up(q, n, xpar, c, upar, w):
                if not (isinstance(q, int) and q < 2):
                    pe.wait_ge(hw_ok, q - 1)
                if c == 0:
                    pe.wait_ge(xT_hi_ok, n + 1)
                    pe.wait_ge(xT_lo_ok, n + 1)
                parts = [(xT_hi, t, low) for t in range(NT) for low in (0, 1)] + [(xT_lo, t, 0) for t in range(NT)]
                for i, (xp, t, low) in enumerate(parts):
                    for half in range(2):
                        a = (2 * c + half) * CF
                        mm = pe.matmul(U[upar][:, half, 0:CF], xp[:, xpar, t, :], w(low, t, a, a + CF),
                                       start=(i == 0), stop=(i == len(parts) - 1))
                mm.then_inc(up_ps, 1)

            def turn_h(q, par):
                pe.wait_ge(hw_ok, q + 1)
                if not (isinstance(q, int) and q == 0):
                    pe.wait_ge(hT_lo_ok, q)
                for k in range(KT):
                    mm = turn(HT[:, k * P:(k + 1) * P], hw[:, par, k * P:(k + 1) * P])
                mm.then_inc(hT_ps, 1)

            def down(q, c, chunks, w, free):
                pe.wait_ge(hT_lo_ok, q + 1)
                if free:
                    pe.wait_ge(*free)
                for k in range(KT):
                    for i, (h, low) in enumerate(((hT_hi, 0), (hT_hi, 1), (hT_lo, 0))):
                        mm = pe.matmul(DN[:, 0:C], h[:, k * P:(k + 1) * P], w(low, c * KT + k),
                                       start=(c == 0 and k == 0 and i == 0),
                                       stop=(c == chunks - 1 and k == KT - 1 and i == 2))
                mm.then_inc(down_ps, 1)

            def kT(b):
                pe.wait_ge(xn2_ok, b + 1)
                for t in range(NT):
                    mm = turn(M1[:, t * P:(t + 1) * P], xn2[:, t * P:(t + 1) * P])
                mm.then_inc(kT_ps, 1)

            def yT(b):
                pe.wait_ge(y_ok, b + 1)
                for t in range(NT):
                    mm = turn(M1[:, t * P:(t + 1) * P], yt[:, t, :])
                mm.then_inc(yT_ps, 1)

            def tile0(b, par, first, last):
                for c in range(CH0):
                    q = CH0 * b + c
                    up(q, b, par, c, c % 2, up0)
                    if first and c == 0:
                        places(0)
                    if c >= 2 or not first:
                        at = (c - 2) % CH0
                        down(q - 2, at, CH0, down0, (x2_ok, b) if at == 0 and not first else None)
                    if c == 2 and not first:
                        kT(b - 1)
                    if c > 0 or not first:
                        turn_h(q - 1, (c - 1) % 2)
                    if c == 1:
                        pre(b + 1)
                    if c == 2:
                        logits(b + 1, 1 - par, wg1 if last else wg0, LG1 if last else LG)
                    if c == CH0 - 1:
                        if not last:
                            places(b + 1)
                        if not first:
                            yT(b - 1)

            pre(0)
            logits(0, 0, wg0, LG)
            pe.wait_ge(s0_lo, NHG * SL)
            tile0(0, 0, True, False)
            with pe.Fori(0, (B - 2) // 2) as i:
                for k in range(2):
                    tile0(2 * i + (k + 1), 1 - k, False, False)
            tile0(B - 1, 1, False, True)

            def tile1(b, par, first, last):
                for c in range(CH1):
                    q = CH1 * b + (Q1 + c)
                    upar = (CH1 * par + c) % 2
                    up(q, b + B, par, c, upar, up1)
                    if c < 2 and first:
                        down(q - 2, c + CH0 - 2, CH0, down0, None)
                    else:
                        if first and c == 2:
                            pe.wait_ge(s1_lo, NU1 + ND1)
                        at = (c - 2) % CH1
                        down(q - 2, at, CH1, down1, None if at else (x2_ok, B) if first else (x4_ok, b))
                    if first and c == 2:
                        kT(B - 1)
                    turn_h(q - 1, 1 - upar)
                    if c == 1 and not last:
                        pre(b + (B + 1))
                    if c == 2 and not last:
                        logits(b + (B + 1), 1 - par, wg1, LG1)
                    if first and c == CH1 - 1:
                        yT(B - 1)
                if last:
                    down(q - 1, CH1 - 2, CH1, down1, None)
                    turn_h(q, upar)
                    down(q, CH1 - 1, CH1, down1, None)

            pe.wait_ge(s1_lo, NU1)
            tile1(0, 0, True, False)
            with pe.Fori(0, (B - 2) // 2) as i:
                for k in range(2):
                    tile1(2 * i + (k + 1), 1 - k, False, False)
            tile1(B - 1, 1, False, True)

        @block.vector
        def _(dve):
            def after(ins, s, value):
                ins.then_inc(s, 1)
                dve.wait_ge(s, value)
                dve.sem_inc(passed_dve, 1)

            dve.wait_ge(small_in, 16)
            dve.tensor_scalar(umax[:], fs, 0.0, None, ALU.max).then_inc(setup_dve, 1)
            dve.tensor_scalar(umin[:], fs, 0.0, None, ALU.min).then_inc(setup_dve, 1)
            dve.tensor_scalar(tdc[:], td, 80.0, None, ALU.min).then_inc(setup_dve, 1)
            dve.wait_ge(iota_ok, 1)
            dve.tensor_copy(iota0[:], iota_i[:]).then_inc(setup_dve, 1)
            dve.sem_inc(prod_ok, Y0)

            def z_of(hg, h):
                rows = cr[:, 0, :, bass.ds(hg * (HG * HD) + h * HD, HD)]
                dve.tensor_tensor(z[:, 0, h, :].rearrange("p (b i j) -> p b i j", b=B, i=HD),
                                  rows.unsqueeze(3).to_broadcast([P, B, HD, HD]),
                                  rows.unsqueeze(2).to_broadcast([P, B, HD, HD]), ALU.mult).then_inc(z_dve, 1)

            def tap_0(hg, h):
                block0 = dyn(tz[:, :, h, 0:P], hg % 2 if isinstance(hg, int) else hg & 1)
                dve.scalar_tensor_tensor(out=block0, in0=anti[:], scalar=db[:, bass.ds(hg * HG + h, 1)],
                                         in1=block0, op0=ALU.mult, op1=ALU.add).then_inc(toep_ok, 1)

            dve.wait_ge(ctx_in[0], 16)
            for h in range(HG):
                z_of(0, h)
            dve.wait_ge(const_ok, 5)
            dve.wait_ge(toep0_in, 16)
            for h in range(HG):
                tap_0(0, h)

            dve.wait_ge(x_in, 16)
            for b in range(B):
                dve.bn_stats(bstq[:, b, :], xs[:, b, :]).then_inc(qstep, 1)
            dve.wait_ge(qstep, B)
            for b in range(B):
                dve.bn_aggr(mvq[:, b, :], bstq[:, b, :]).then_inc(qstep, 1)
            dve.wait_ge(qstep, 2 * B)
            dve.tensor_scalar(veq[:], mvq[:, :, 1], LN_EPS, None, ALU.add).then_inc(qvar_ok, 1)
            dve.wait_ge(qrstd_ok, 1)
            for b in range(B):
                dve.tensor_scalar(qn[:, b, :], xs[:, b, :], mvq[:, b, 0:1], rsq[:, b:b + 1],
                                  ALU.subtract, ALU.mult).then_inc(qn_ok, 1)
            dve.wait_ge(qT_ok, B)

            def sum_rows(hg, k):
                h, t = k // NT, k % NT
                dve.wait_ge(prod_ok, BLK * hg + (k + 1 + Y0))
                dve.tensor_reduce(oc[:, t, :, bass.ds(hg * (HG * HD) + h * HD, HD)],
                                  prod[:, k % 4, :].rearrange("p (b i j) -> p b j i", b=B, i=HD),
                                  AX.X, ALU.add).then_inc(oc_ok, 1)

            def step(hg, last):
                for k in range(BLK):
                    h, t = k // NT, k % NT
                    dve.wait_ge(conv_ps, BLK * hg + (k + 1))
                    if k >= 4:
                        dve.wait_ge(oc_ok, BLK * hg + (k - 3))
                    q = qt[:, t, :, bass.ds(hg * (HG * HD) + h * HD, HD)]
                    dve.tensor_tensor(prod[:, k % 4, :].rearrange("p (b i j) -> p b i j", b=B, i=HD),
                                      Y[k % Y0].rearrange("p (b i j) -> p b i j", b=B, i=HD),
                                      q.unsqueeze(3).to_broadcast([P, B, HD, HD]), ALU.mult)\
                        .then_inc(prod_ok, 1)
                    if k == 0 and not last:
                        dve.wait_ge(toep_in, 16 * (hg + 1))
                    if t == NT - 1 and not last:
                        z_of(hg + 1, h)
                        tap_0(hg + 1, h)
                    if k > 0:
                        sum_rows(hg, k - 1)
                sum_rows(hg, BLK - 1)
                dve.wait_ge(oc_ok, BLK * (hg + 1))

            with dve.Fori(0, NHG - 1) as hg:
                step(hg, False)
            step(NHG - 1, True)

            def tile_of(b):
                return dyn(xs, b)

            def stats(n, b, ready, count):
                dve.wait_ge(ready, count)
                dve.sem_inc(passed_dve, 1)
                after(dve.bn_stats(bst[:], tile_of(b)), ln_step, 2 * n + 1)
                after(dve.bn_aggr(mv[:], bst[:]), ln_step, 2 * n + 2)
                dve.tensor_scalar(ve[:], mv[:, 1:2], LN_EPS, None, ALU.add).then_inc(var_ok, 1)

            def normed(n, b):
                if not (isinstance(n, int) and n == 0):
                    dve.wait_ge(xT_ps, n)
                dve.wait_ge(rstd_ok, n + 1)
                dve.tensor_scalar(xn[:], tile_of(b), mv[:, 0:1], rs[:, 0:1], ALU.subtract, ALU.mult)\
                    .then_inc(xn_ok, 1)

            def add_conv(b):
                dve.wait_ge(oT_ps, b + 1)
                dve.scalar_tensor_tensor(out=xs[:, b, :], in0=M[b % 4][:, 0:C], scalar=gt[:, 0:1],
                                         in1=xs[:, b, :], op0=ALU.mult, op1=ALU.add).then_inc(x1_ok, 1)

            dve.wait_ge(setup_act, 5)
            add_conv(0)
            stats(0, 0, x1_ok, 1)
            add_conv(1)
            add_conv(2)
            normed(0, 0)
            for b in range(3, B):
                add_conv(b)
            dve.memset(run[:], 0.0).then_inc(run_ok, 1)
            dve.memset(sa[:, :, 0:1], 0.0).then_inc(pad_ok, 1)
            dve.memset(sb_[:, :, 0:1], 1.0).then_inc(pad_ok, 1)
            dve.memset(g[:, :, E0:ES0], 1.0).then_inc(pad_ok, 1)
            dve.memset(hw[:, :, CF:CP], 0.0).then_inc(pad_ok, 1)
            dve.wait_ge(pad_ok, 4)

            def best(top, experts, at):
                after(dve.max(v8[:], sc[:, 0:experts]), route, at + 1)
                after(dve.max_index(i8[:], v8[:], sc[:, 0:experts]), route, at + 2)
                after(dve.tensor_copy(f8[:], i8[:]), route, at + 3)
                dve.tensor_tensor(eq[:, 0:top, 0:experts],
                                  iota0[:, 0:experts].unsqueeze(1).to_broadcast([P, top, experts]),
                                  f8[:, 0:top].unsqueeze(2).to_broadcast([P, top, experts]),
                                  ALU.is_equal).then_inc(route, 1)

            def chosen(top, experts, at):
                dve.wait_ge(route, at + 4)
                after(dve.tensor_reduce(mask[:, 0:experts], eq[:, 0:top, 0:experts].rearrange("p k e -> p e k"),
                                        AX.X, ALU.add), route, at + 5)

            def route0(b):
                at = RT0 * b
                dve.wait_ge(exp_ok, b + 1)
                after(dve.tensor_scalar(sc[:], es0[:], 1.0, None, ALU.add), route, at + 1)
                after(dve.reciprocal(sc[:], sc[:]), route, at + 2)
                best(TOP0, E0, at + 2)

            def chosen0(b):
                chosen(TOP0, E0, RT0 * b + 2)
                dve.tensor_copy(maskb[:], mask[:]).then_inc(mask_ok, 1)

            def scores0(b):
                at = RT0 * b + 7
                dve.tensor_tensor(msc[:], mask[:], sc[:], ALU.mult).then_inc(route, 1)
                dve.tensor_reduce(den[:], v8[:, 0:TOP0], AX.X, ALU.add).then_inc(route, 1)
                dve.wait_ge(route, at + 2)
                dve.reciprocal(rden[:], den[:]).then_inc(route, 1)

            def weights0(b, par):
                at = RT0 * b + 10
                dve.wait_ge(pos_ps, b + 1)
                if not (isinstance(b, int) and b == 0):
                    dve.wait_ge(hw_ok, CH0 * b - CH0 + 1)
                dve.wait_ge(route, at)
                after(dve.scalar_tensor_tensor(out=g[:, par, 0:E0], in0=PS, scalar=float(CAP0), in1=msc[:],
                                               op0=ALU.is_lt, op1=ALU.mult), route, at + 1)
                dve.tensor_scalar(g[:, par, 0:E0], g[:, par, 0:E0], rden[:, 0:1], None, ALU.mult).then_inc(g_ok, 1)
                dve.tensor_tensor(run[:], run[:], maskb[:], ALU.add).then_inc(run_ok, 1)

            def logit_max(b):
                dve.wait_ge(lg_ps, b + (B + 1))
                dve.tensor_reduce(nmx[:], LG1, AX.X, ALU.max, negate=True).then_inc(nmx_ok, 1)

            def route1(b, par):
                at = RT1 * b + RT0 * B
                dve.wait_ge(exp_ok, b + (B + 1))
                after(dve.tensor_reduce(den[:], es0[:, 0:E1], AX.X, ALU.add), route, at + 1)
                after(dve.reciprocal(rden[:], den[:]), route, at + 2)
                after(dve.tensor_scalar(sc[:, 0:E1], es0[:, 0:E1], rden[:, 0:1], None, ALU.mult), route, at + 3)
                best(TOP1, E1, at + 3)
                chosen(TOP1, E1, at + 3)
                dve.tensor_tensor(msc[:, 0:E1], mask[:, 0:E1], sc[:, 0:E1], ALU.mult).then_inc(route, 1)
                dve.tensor_reduce(den[:], v8[:, 0:TOP1], AX.X, ALU.add).then_inc(route, 1)
                dve.wait_ge(route, at + 10)
                after(dve.reciprocal(rden[:], den[:]), route, at + 11)
                dve.tensor_scalar(g[:, par, 0:E1], msc[:, 0:E1], rden[:, 0:1], None, ALU.mult).then_inc(g_ok, 1)

            def act0(q, par):
                dve.wait_ge(sil_ok, q + 1)
                if not (isinstance(q, int) and q == 0):
                    dve.wait_ge(hw_ok, q)
                dve.tensor_tensor(av[:], sil[:], U[par][:, 1, 0:CF], ALU.mult).then_inc(av_ok, 1)

            def act1(q, c, par, gpar):
                dve.wait_ge(sil_ok, q + 1)
                dve.wait_ge(hT_ps, q - 1)
                if c < CH1 - 1:
                    for e in range(2):
                        a = e * H1
                        ins = dve.scalar_tensor_tensor(out=hw[:, par, a:a + H1], in0=sil[:, a:a + H1],
                                                       scalar=g[:, gpar, 2 * c + e:2 * c + e + 1],
                                                       in1=U[par][:, 1, a:a + H1], op0=ALU.mult, op1=ALU.mult)
                else:
                    ins = dve.tensor_tensor(hw[:, par, 0:CF], sil[:], U[par][:, 1, 0:CF], ALU.mult)
                ins.then_inc(hw_ok, 1)

            def low(q):
                dve.wait_ge(hT_hi_ok, q + 1)
                dve.tensor_tensor(hT_lo[:], HT[:, 0:CP], hT_hi[:].bitcast(F32), ALU.subtract).then_inc(hT_lo_ok, 1)

            def add(q, b, gate, done):
                dve.wait_ge(down_ps, q)
                dve.scalar_tensor_tensor(out=tile_of(b), in0=DN[:, 0:C], scalar=gt[:, gate:gate + 1],
                                         in1=tile_of(b), op0=ALU.mult, op1=ALU.add).then_inc(done, 1)

            def stats2(b):
                dve.wait_ge(x2_ok, b + 1)
                dve.sem_inc(passed_dve, 1)
                after(dve.bn_stats(bst2[:], tile_of(b)), ln2_step, 2 * b + 1)

            def variance2(b):
                after(dve.bn_aggr(mv2[:], bst2[:]), ln2_step, 2 * b + 2)
                dve.tensor_scalar(ve2[:], mv2[:, 1:2], LN_EPS, None, ALU.add).then_inc(var2_ok, 1)

            def normed2(b):
                dve.wait_ge(rstd2_ok, b + 1)
                dve.tensor_scalar(xn2[:], tile_of(b), mv2[:, 0:1], rs2[:, 0:1], ALU.subtract, ALU.mult)\
                    .then_inc(xn2_ok, 1)

            def scan(b, dst, src, ready):
                dve.wait_ge(*ready)
                for t in range(NT):
                    dve.tensor_tensor_scan(dst[:, t, 1:R + 1], dc[:, t:t + 1].to_broadcast([P, R]),
                                           src[:, t, :], 0.0, ALU.mult, ALU.add).then_inc(wk, 1)

            def with_own(b, own, s, count):
                dve.wait_ge(pk, PK * b + count)
                for t in range(NT):
                    dve.scalar_tensor_tensor(out=own[:, t, :], in0=own[:, t, :], scalar=c2[:, t:t + 1],
                                             in1=s[:, t, 0:R], op0=ALU.mult, op1=ALU.add).then_inc(wk, 1)

            def inverse(b, t):
                dve.wait_ge(wk, WK * b + 5 + t)
                dve.reciprocal(ek[:, t, :], ek[:, t, :]).then_inc(wk, 1)

            def add_y(b):
                dve.wait_ge(yT_ps, b + 1)
                dve.scalar_tensor_tensor(out=tile_of(b), in0=M1[:, 0:C], scalar=gt[:, 1:2],
                                         in1=tile_of(b), op0=ALU.mult, op1=ALU.add).then_inc(x3_ok, 1)

            def tile0(b, par, first, last):
                q = CH0 * b
                if last:
                    stats(B, 0, x3_ok, 1)
                else:
                    stats(b + 1, b + 1, x1_ok, B)
                act0(q, 0)
                if last:
                    normed(B, 0)
                else:
                    normed(b + 1, b + 1)
                if not first:
                    low(q - 1)
                act0(q + 1, 1)
                if not first:
                    add(q, b - 1, 2, x2_ok)
                    stats2(b - 1)
                low(q)
                if not first:
                    variance2(b - 1)
                    normed2(b - 1)
                act0(q + 2, 0)
                low(q + 1)
                if last:
                    logit_max(0)
                act0(q + 3, 1)
                if not first:
                    scan(b - 1, sb_, ek, (ek_ok, b))
                low(q + 2)
                if not last:
                    route0(b + 1)
                else:
                    route1(0, 1 - par)
                if not first:
                    scan(b - 1, sa, ev, (ev_ok, b))
                act0(q + 4, 0)
                low(q + 3)
                if not last:
                    chosen0(b + 1)
                if not first:
                    with_own(b - 1, ek, sb_, 1)
                    inverse(b - 1, 0)
                    with_own(b - 1, ev, sa, 2)
                act0(q + 5, 1)
                if not first:
                    inverse(b - 1, 1)
                if not last:
                    scores0(b + 1)
                low(q + 4)
                if not last:
                    weights0(b + 1, 1 - par)
                if not first:
                    add_y(b - 1)

            route0(0)
            chosen0(0)
            scores0(0)
            weights0(0, 0)
            tile0(0, 0, True, False)
            with dve.Fori(0, (B - 2) // 2) as i:
                for k in range(2):
                    tile0(2 * i + (k + 1), 1 - k, False, False)
            tile0(B - 1, 1, False, True)

            def tile1(b, par, first, last):
                q = CH1 * b + Q1
                last_b = B - 1
                if not last:
                    stats(b + (B + 1), b + 1, x3_ok, b + 2)
                act1(q, 0, CH1 * par % 2, par)
                if not last:
                    normed(b + (B + 1), b + 1)
                low(q - 1)
                act1(q + 1, 1, (CH1 * par + 1) % 2, par)
                if first:
                    add(q, last_b, 2, x2_ok)
                    stats2(last_b)
                else:
                    add(q, b - 1, 3, x4_ok)
                low(q)
                if first:
                    variance2(last_b)
                    normed2(last_b)
                act1(q + 2, 2, (CH1 * par) % 2, par)
                low(q + 1)
                if not last:
                    logit_max(b + 1)
                act1(q + 3, 3, (CH1 * par + 1) % 2, par)
                if first:
                    scan(last_b, sb_, ek, (ek_ok, B))
                    scan(last_b, sa, ev, (ev_ok, B))
                low(q + 2)
                if not last:
                    route1(b + 1, 1 - par)
                if first:
                    with_own(last_b, ek, sb_, 1)
                    inverse(last_b, 0)
                    with_own(last_b, ev, sa, 2)
                act1(q + 4, 4, (CH1 * par) % 2, par)
                if first:
                    inverse(last_b, 1)
                low(q + 3)
                if first:
                    add_y(last_b)
                if last:
                    low(q + 4)
                    add(q + CH1, b, 3, x4_ok)

            tile1(0, 0, True, False)
            with dve.Fori(0, (B - 2) // 2) as i:
                for k in range(2):
                    tile1(2 * i + (k + 1), 1 - k, False, False)
            tile1(B - 1, 1, False, True)


_SHAPE = (B, R, C)


def kernel(x, ctx_2048, g_xattn, g_ffn, L0_xattn_ssm_kernel, L0_xattn_D, L0_ffn_w_gate, L0_ffn_w_shared_up,
           L0_ffn_w_shared_down, L0_ffn_w_up, L0_ffn_w_down, L1_xattn_time_decay, L1_xattn_time_first,
           L1_ffn_gate_weight, L1_ffn_w_gate, L1_ffn_w_up, L1_ffn_w_down, L1_ffn_w_shared_gate,
           L1_ffn_w_shared_up, L1_ffn_w_shared_down):
    import numpy as np
    import concourse.bacc as bacc
    from concourse.bass_utils import run_bass_kernel_spmd as run

    f32 = np.float32

    def channels_first(a):
        return a.reshape(NT, P, -1).transpose(1, 0, 2).reshape(P, -1)

    def rows_first(a):
        return a.reshape(-1, P, C).transpose(1, 0, 2).reshape(P, -1)

    x = np.asarray(x)
    ctx = np.asarray(ctx_2048).transpose(2, 0, 1).reshape(NT, P, B, R)
    ctx_t = ctx.transpose(1, 0, 2, 3)
    ctx_rev = ctx[:, ::-1].transpose(1, 0, 2, 3)
    taps = np.asarray(L0_xattn_ssm_kernel)
    conv_pad = np.concatenate([np.zeros((HEADS, P - 1), f32), taps, np.zeros((HEADS, 1), f32)], axis=1)

    def gate_value(gate, value, chunks):
        both = np.stack([gate.reshape(C, chunks, CF), value.reshape(C, chunks, CF)], axis=2)
        return channels_first(both.reshape(C, -1))

    def padded_rows(w, chunks):
        w = np.concatenate([w.reshape(chunks, CF, C), np.zeros((chunks, CP - CF, C), f32)], axis=1)
        return rows_first(w)

    up0, sh0 = np.asarray(L0_ffn_w_up), np.asarray(L0_ffn_w_shared_up)
    w0 = np.concatenate([
        gate_value(np.concatenate([up0[:, :, :H0].transpose(1, 0, 2).reshape(C, -1), sh0[:, HS0:]], axis=1),
                   np.concatenate([up0[:, :, H0:].transpose(1, 0, 2).reshape(C, -1), sh0[:, :HS0]], axis=1), CH0),
        padded_rows(np.concatenate([np.asarray(L0_ffn_w_down).reshape(-1, C), np.asarray(L0_ffn_w_shared_down)]), CH0),
    ], axis=1)
    gate1 = np.concatenate([np.asarray(L1_ffn_w_gate).reshape(-1, C), np.asarray(L1_ffn_w_shared_gate)]).T
    value1 = np.concatenate([np.asarray(L1_ffn_w_up).reshape(-1, C), np.asarray(L1_ffn_w_shared_up)]).T
    down1 = np.concatenate([np.asarray(L1_ffn_w_down).transpose(0, 2, 1).reshape(-1, C),
                            np.asarray(L1_ffn_w_shared_down).T])
    w1 = np.concatenate([gate_value(gate1, value1, CH1), padded_rows(down1, CH1)], axis=1)

    def on_all(a):
        return np.broadcast_to(np.asarray(a).reshape(1, -1), (P, np.size(a)))

    small = np.concatenate([
        on_all(L0_xattn_D), on_all(g_xattn), on_all(g_ffn),
        np.asarray(L1_xattn_time_decay).reshape(NT, P).T, np.asarray(L1_xattn_time_first).reshape(NT, P).T,
        channels_first(np.asarray(L0_ffn_w_gate)), channels_first(np.asarray(L1_ffn_gate_weight).T),
    ], axis=1)

    arrays = {"small": small, "x": x, "ctx_t": ctx_t, "ctx_rev": ctx_rev, "conv_pad": conv_pad, "w0": w0, "w1": w1}
    arrays = {f"in_{k}": np.ascontiguousarray(v) for k, v in arrays.items()}
    nc = bacc.Bacc("TRN2", target_bir_lowering=False, num_devices=1)
    args = [nc.dram_tensor(k, v.shape, F32, kind="ExternalInput").ap() for k, v in arrays.items()]
    args.append(nc.dram_tensor("out_x", _SHAPE, F32, kind="ExternalOutput").ap())
    build(nc, *args)
    r = run(nc, [arrays], core_ids=[0])
    return r.results[0]["out_x"]
```

```python
from contextlib import ExitStack

import concourse.bass as bass
from concourse import mybir

F32 = mybir.dt.float32
F32R = mybir.dt.float32r
BF16 = mybir.dt.bfloat16
U32 = mybir.dt.uint32
I32 = mybir.dt.int32
ALU = mybir.AluOpType
ACT = mybir.ActivationFunctionType
AX = mybir.AxisListType

P = 128
B, R, C = 8, 128, 256
NT = C // P
HEADS, HD = 16, 8
HG = 4
NHG = HEADS // HG
HB = B // 2
KW = HD * HD
BLK = NT * HG
LN_EPS = 1e-5

KT = 3
CP = KT * P

E0, H0, TOP0, CAP0, HS0 = 64, 32, 6, 128, 64
ES0 = E0 + HS0 // H0
CE0 = CP // H0
WD0 = [min(CE0, ES0 - a) * H0 for a in range(0, ES0, CE0)]
CH0 = len(WD0)
UW0 = 2 * sum(WD0)
NK0 = sum(-(-w // P) for w in WD0)

E1, H1, TOP1, HS1 = 8, 176, 2, 352
ES1 = E1 + HS1 // H1
CF1 = CP // ES1
WD1 = [ES1 * min(CF1, H1 - a) for a in range(0, H1, CF1)]
CH1 = len(WD1)
UW1 = 2 * sum(WD1)
NK1 = sum(-(-w // P) for w in WD1)
Q1 = CH0 * B

L0 = 4
W0 = NT * UW0 + NK0 * C
NP0 = 16
PC0 = W0 // NP0
NPZ, NPL = 1, 7
GR1 = 4
NU1 = GR1 * B
PCU1 = NT * UW1 // NU1
ND1 = NK1
DPR = 3 * KT
D1_OVER = -(-DPR * C // (2 * CP))
DP0 = ND1 - KT - 2
DOWNS0 = [list(range(a, b)) for a, b in ((0, 0), (0, 0), (0, 3), (3, 5), (5, 7), (7, DP0))]
Z0_POOL = (0, 1, 2, 3)
LAG = 3
Q_END = Q1 + CH1 * B
DOWNS1 = [list(range(DP0 + a, DP0 + b)) for a, b in ((0, 1), (1, 3), (3, ND1 - DP0), (0, 0), (0, 0))]
PIECES0 = (1, 2, 4, 5)
SPLITS0 = (0, 1, 3, 4)

RT0, RT1 = 11, 11
EK, EV, WK = 4, 2, 8
Y0 = 4

S_GATE, S_TD, S_FS = 0, 4, 4 + NT
S_WG0 = S_FS + NT
S_WG1 = S_WG0 + NT * E0
SMALL = S_WG1 + NT * E1


def build(nc, small_d, x, ctx_t, ctx_rev, conv_pad, w0, w1, taps_d, out):
    es = ExitStack()
    with es:
        def sb(name, shape, dt=F32, stack=es):
            return stack.enter_context(nc.sbuf_tensor(name, shape, dt))

        def pb(name, shape):
            return es.enter_context(nc.psum_tensor(name, shape, F32))

        def sem(name):
            return es.enter_context(nc.semaphore(name))

        small = sb("small", [P, SMALL])
        gates_sb = small[:, S_GATE:S_GATE + 4]
        td = small[:, S_TD:S_TD + NT]
        fs = small[:, S_FS:S_FS + NT]
        wg0 = small[:, S_WG0:S_WG1].rearrange("p (t e) -> p t e", t=NT)
        wg1 = small[:, S_WG1:SMALL].rearrange("p (t e) -> p t e", t=NT)
        xs = sb("xs", [P, B, C])
        w0_hi = sb("w0_hi", [P, NT * UW0 + NK0 * C], F32R)
        w0_in_place = ExitStack()
        w0_raw = sb("w0_raw", [P, W0], stack=w0_in_place)
        w0_in_place.close()
        w0_lo = sb("w0_lo", [P, W0], F32R)
        ident = sb("ident", [P, P])
        tri = sb("tri", [P, P], BF16)
        ones = sb("ones", [P, P], BF16)
        iota0 = sb("iota0", [P, E0])
        nhalf = sb("nhalf", [P, B])
        gt = sb("gt", [P, 4])
        tdc = sb("tdc", [P, NT])
        etd = sb("etd", [P, NT])
        dc = sb("dc", [P, NT])
        nmax = sb("nmax", [P, NT])
        umin = sb("umin", [P, NT])
        bst = sb("bst", [P, 6])
        mv = sb("mv", [P, 2])
        ve = sb("ve", [P, 1])
        rs = sb("rs", [P, 1])
        xn = sb("xn", [P, C])

        a_stage = ExitStack()
        padded = sb("padded", [HEADS, 3 * P + 1], stack=a_stage)
        bstq = sb("bstq", [P, B, 6], stack=a_stage)
        mvq = sb("mvq", [P, B, 2], stack=a_stage)
        veq = sb("veq", [P, B], stack=a_stage)
        rsq = sb("rsq", [P, B], stack=a_stage)
        iota_i = sb("iota_i", [P, E0], I32, stack=a_stage)
        tz = sb("tz", [P, 2, HG, 2 * P], stack=a_stage)
        z = sb("z", [P, NT, HG, B * KW], stack=a_stage)
        qt = sb("qt", [P, NT, B, R], stack=a_stage)
        prod = sb("prod", [P, 4, B * KW], stack=a_stage)
        oc = sb("oc", [P, NT, B, R], stack=a_stage)
        cr = sb("cr", [P, NT, B, R], stack=a_stage)
        qn = oc[:].rearrange("p t b r -> p (t b r)").rearrange("p (b c) -> p b c", b=B)
        a_stage.close()

        w1u_hi = sb("w1u_hi", [P, NT * UW1], F32R)
        w1_in_place = ExitStack()
        w1_raw = sb("w1_raw", [P, NT * UW1], stack=w1_in_place)
        w1_in_place.close()
        w1u_lo = sb("w1u_lo", [P, NT * UW1], F32R)
        ct = sb("ct", [P, NT, B, R])
        sil = sb("sil", [P, CP])
        av = sb("av", [P, CP])
        hw = sb("hw", [P, 2, CP])
        hT_hi = sb("hT_hi", [P, 2, CP], F32R)
        hT_lo = sb("hT_lo", [P, 2, CP], F32R)
        ek = sb("ek", [P, NT, R])
        ev = sb("ev", [P, NT, R])
        own_k = sb("own_k", [P, NT, R])
        own_v = sb("own_v", [P, NT, R])
        sa = sb("sa", [P, NT, R + 1])
        sb_ = sb("sb_", [P, NT, R + 1])
        xn2 = sb("xn2", [P, C])
        yt = xn2[:, :].rearrange("p (t r) -> p t r", t=NT)
        eq = sb("eq", [P, TOP0, E0])
        xT = sb("xT", [P, NT, R])
        xT_hi = sb("xT_hi", [P, 2, NT, R], F32R)
        xT_lo = sb("xT_lo", [P, 2, NT, R], F32R)
        es0 = sb("es0", [P, E0])
        sc = sb("sc", [P, E0])
        v8 = sb("v8", [P, 8])
        i8 = sb("i8", [P, 8], U32)
        f8 = sb("f8", [P, 8])
        mask = sb("mask", [P, E0])
        maskb = sb("maskb", [P, E0], BF16)
        run = sb("run", [P, E0], BF16)
        den = sb("den", [P, 1])
        rden = sb("rden", [P, 1])
        msc = sb("msc", [P, E0])
        g = sb("g", [P, 2, ES0])
        nmx = sb("nmx", [P, 1])
        bst2 = sb("bst2", [P, 6])
        mv2 = sb("mv2", [P, 2])
        ve2 = sb("ve2", [P, 1])
        rs2 = sb("rs2", [P, 1])

        U = [pb(f"U{i}", [P, 2, 512]) for i in range(2)]
        HT = [pb(f"HT{i}", [P, 512]) for i in range(2)]
        DN = pb("DN", [P, 512])
        M0 = pb("M0", [P, 512])
        Y = [U[0][:, 0, :], U[0][:, 1, :], U[1][:, 0, :], U[1][:, 1, :]]
        M = [M0, HT[0], HT[1], DN] + Y
        TURN, LG, PS = M0[:, 0:C], M0[:, C:C + E0], M0[:, C + E0:C + 2 * E0]
        g1 = g[:, :, E0 - E1:E0 - E1 + ES1]
        LG1 = M0[:, C:C + E1]

        def up0(low, t, a, b):
            return (w0_hi, w0_lo)[low][:, t * UW0 + a:t * UW0 + b]

        def up1(low, t, a, b):
            return (w1u_hi, w1u_lo)[low][:, t * UW1 + a:t * UW1 + b]

        def down0(low, k):
            return (w0_hi, w0_lo)[low][:, NT * UW0 + k * C:NT * UW0 + (k + 1) * C]

        def down1_at(k):
            return (k // DPR) * UW0 + (k % DPR) * C

        def down1(low, k):
            return (w0_hi, w0_lo)[low][:, down1_at(k):down1_at(k) + C]

        ctx_in = [sem(f"ctx_in{i}") for i in range(NT)]
        x_in = [sem(f"x_in{i}") for i in range(2)]
        small_in, ct_in, out_done = sem("small_in"), sem("ct_in"), sem("out_done")
        toep0_in, toep_in = sem("toep0_in"), sem("toep_in")
        w0_in = [sem(f"w0_in{i}") for i in range(L0)]
        w1_in = [sem(f"w1_in{i}") for i in range(L0)]
        down1_in = [sem(f"down1_in{j}") for j in range(CH1)]
        pad_in, with_d, taps_out = sem("pad_in"), sem("with_d"), sem("taps_out")
        memset_ok, const_ok, iota_ok = sem("memset_ok"), sem("const_ok"), sem("iota_ok")
        passed_dve, passed_pool = sem("passed_dve"), sem("passed_pool")
        setup_dve, setup_act = sem("setup_dve"), sem("setup_act")
        s0_hi, s0_lo = sem("s0_hi"), sem("s0_lo")
        s1_hi, s1_lo = sem("s1_hi"), sem("s1_lo")
        qstep, qvar_ok, qrstd_ok, qn_ok = sem("qstep"), sem("qvar_ok"), sem("qrstd_ok"), sem("qn_ok")
        qT_ps, qT_ok = sem("qT_ps"), sem("qT_ok")
        z_dve, z_pool, z0_pool = sem("z_dve"), sem("z_pool"), sem("z0_pool")
        conv_ps, oc_ok = sem("conv_ps"), sem("oc_ok")
        prod_ok = sem("prod_ok")
        oT_ps, x1_ok = sem("oT_ps"), sem("x1_ok")
        ln_step, var_ok, rstd_ok, xn_ok = sem("ln_step"), sem("var_ok"), sem("rstd_ok"), sem("xn_ok")
        xT_ps, xT_ok, xT_hi_ok, xT_lo_ok = sem("xT_ps"), sem("xT_ok"), sem("xT_hi_ok"), sem("xT_lo_ok")
        lg_ps, nmx_ok, exp_ok, route, mask_ok = sem("lg_ps"), sem("nmx_ok"), sem("exp_ok"), sem("route"), sem("mask_ok")
        pos_ps, g_ok, run_ok = sem("pos_ps"), sem("g_ok"), sem("run_ok")
        up_ps, sil_ok, av_ok, hw_ok = sem("up_ps"), sem("sil_ok"), sem("av_ok"), sem("hw_ok")
        hT_ps, hT_hi_ok, hT_lo_ok, down_ps = sem("hT_ps"), sem("hT_hi_ok"), sem("hT_lo_ok"), sem("down_ps")
        x2_ok, x4_ok, pad_ok, hpad_ok = sem("x2_ok"), sem("x4_ok"), sem("pad_ok"), sem("hpad_ok")
        ln2_step, var2_ok, rstd2_ok, xn2_ok = sem("ln2_step"), sem("var2_ok"), sem("rstd2_ok"), sem("xn2_ok")
        kT_ps, ek_ok, ev_ok, wk = sem("kT_ps"), sem("ek_ok"), sem("ev_ok"), sem("wk")
        y_ok, yT_ps, x3_ok = sem("y_ok"), sem("yT_ps"), sem("x3_ok")

        block = es.enter_context(nc.Block())

        def tiles(width):
            return -(-width // P)

        def width0(j, last=False):
            return WD0[j] if j < CH0 else (WD1 if last else WD0)[j - CH0]

        def width1(j):
            return WD1[j % CH1]

        def pieces0(columns):
            return -(-columns // PC0)

        def z_dve_count(hg, h):
            own = [i for i in range(HG) if i not in Z0_POOL]
            return HG + len(own) * (hg - 1) + own.index(h) + 1 if hg else h + 1

        def dyn(t, b):
            if isinstance(b, int):
                return t[:, b]
            return t[:, bass.ds(b, 1)].rearrange("p o c -> p (o c)")

        def ctx_of(b):
            if isinstance(b, int):
                return ct[:, :, b, :]
            return ct[:, :, bass.ds(b, 1), :].rearrange("p t o r -> p t (o r)")

        @block.sync
        def _(sp):
            def toeplitz(hg, signal):
                src = bass.AP(taps_d.tensor, hg * (HG * 3 * P), [[1, P], [3 * P, HG], [1, 2 * P]])
                sp.dma_start(tz[:, hg % 2], src).then_inc(signal, 16)

            sp.dma_start(padded[:], conv_pad).then_inc(pad_in, 16)
            sp.dma_start(cr[:, 0], ctx_rev[:, 0]).then_inc(ctx_in[0], 16)
            sp.wait_ge(with_d, 1)
            sp.dma_start(taps_d, padded[:, 0:3 * P]).then_inc(taps_out, 16)
            for i in range(2):
                half = slice(i * HB, (i + 1) * HB)
                sp.dma_start(xs[:, half], x[half].rearrange("b r c -> r b c")).then_inc(x_in[i], 16)
            sp.wait_ge(taps_out, 16)
            toeplitz(0, toep0_in)
            sp.dma_start(small[:], small_d).then_inc(small_in, 16)
            sp.dma_start(cr[:, 1], ctx_rev[:, 1]).then_inc(ctx_in[1], 16)
            toeplitz(1, toep_in)
            for i in range(L0):
                part = slice(i * W0 // L0, (i + 1) * W0 // L0)
                sp.dma_start(w0_raw[:, part], w0[:, part]).then_inc(w0_in[i], 16)
            for hg in range(2, NHG):
                sp.wait_ge(toep_in, 16 * (hg - 1))
                sp.wait_ge(conv_ps, BLK * (hg - 1))
                toeplitz(hg, toep_in)
            sp.wait_ge(x1_ok, B)
            for i in range(L0):
                part = slice(i * NT * UW1 // L0, (i + 1) * NT * UW1 // L0)
                sp.dma_start(w1_raw[:, part], w1[:, part]).then_inc(w1_in[i], 16)
                if i == 0:
                    sp.dma_start(ct[:], ctx_t).then_inc(ct_in, 16)
            sp.wait_ge(up_ps, CH0 * (B - 1) + D1_OVER)
            for j in range(CH1):
                at, src, n = down1_at(KT * j), NT * UW1 + KT * j * C, tiles(WD1[j]) * C
                sp.dma_start(w0_raw[:, at:at + n], w1[:, src:src + n])\
                    .then_inc(down1_in[j], 16)
            with sp.Fori(0, B) as b:
                sp.wait_ge(x4_ok, b + 1)
                sp.dma_start(out[bass.ds(b, 1)].rearrange("b r c -> r (b c)"), dyn(xs, b)).then_inc(out_done, 16)
            sp.wait_ge(out_done, 16 * B)

        @block.gpsimd
        def _(pool):
            pool.memset(ident[:], 0.0).then_inc(memset_ok, 1)
            pool.memset(tri[:], 1.0).then_inc(memset_ok, 1)
            pool.memset(ones[:], 1.0).then_inc(const_ok, 1)
            pool.memset(nhalf[:], -0.5).then_inc(const_ok, 1)
            pool.iota(iota_i[:], [[1, E0]], base=0, channel_multiplier=0).then_inc(iota_ok, 1)
            pool.wait_ge(memset_ok, 2)
            pool.affine_select(out=ident[:], in_=ident[:], compare_op=ALU.not_equal, fill=1.0, base=0,
                               pattern=[[-1, P]], channel_multiplier=1).then_inc(const_ok, 1)
            pool.affine_select(out=tri[:], in_=tri[:], compare_op=ALU.is_gt, fill=0.0, base=0,
                               pattern=[[1, P]], channel_multiplier=-1).then_inc(const_ok, 1)
            pool.wait_ge(const_ok, 4)

            def z_of(t, hg, h, signal):
                rows = cr[:, t, :, bass.ds(hg * (HG * HD) + h * HD, HD)]
                pool.tensor_tensor(z[:, t, h, :].rearrange("p (b i j) -> p b i j", b=B, i=HD),
                                   rows.unsqueeze(3).to_broadcast([P, B, HD, HD]),
                                   rows.unsqueeze(2).to_broadcast([P, B, HD, HD]), ALU.mult).then_inc(signal, 1)

            def low0(m):
                pool.wait_ge(s0_hi, m + 1)
                at = bass.ds(m * PC0, PC0)
                pool.tensor_tensor(w0_lo[:, at], w0_raw[:, at], w0_hi[:, at].bitcast(F32),
                                   ALU.subtract).then_inc(s0_lo, 1)

            for i in range(2):
                half = slice(i * HB, (i + 1) * HB)
                pool.wait_ge(qvar_ok, i + 1)
                pool.tensor_tensor(rsq[:, half], veq[:, half], nhalf[:, half], ALU.pow).then_inc(qrstd_ok, 1)
            pool.wait_ge(ctx_in[1], 16)
            for h in range(HG):
                z_of(1, 0, h, z_pool)
            pool.wait_ge(ctx_in[0], 16)
            with pool.Fori(0, NHG - 1) as hg:
                for h in range(HG):
                    pool.wait_ge(conv_ps, BLK * hg + NT * (h + 1))
                    z_of(1, hg + 1, h, z_pool)
                    if h in Z0_POOL:
                        z_of(0, hg + 1, h, z0_pool)
                    if h < NPZ:
                        low0(NPZ * hg + h)
            for m in range(NPZ * (NHG - 1), NP0 - NPL):
                low0(m)

            def rstd(n):
                pool.wait_ge(var_ok, n + 1)
                pool.tensor_tensor(rs[:], ve[:], nhalf[:, 0:1], ALU.pow).then_inc(rstd_ok, 1)

            def rstd2(b):
                pool.wait_ge(var2_ok, b + 1)
                pool.tensor_tensor(rs2[:], ve2[:], nhalf[:, 0:1], ALU.pow).then_inc(rstd2_ok, 1)

            def xT_low(n, par):
                pool.wait_ge(xT_hi_ok, n + 1)
                pool.tensor_tensor(xT_lo[:, par], xT[:], xT_hi[:, par].bitcast(F32), ALU.subtract)\
                    .then_inc(xT_lo_ok, 1)

            def weigh(q, par, weights, experts, width):
                pool.wait_ge(av_ok, q + 1)
                if not (isinstance(q, int) and q < 2):
                    pool.wait_ge(hT_ps, q - 1)
                pool.tensor_tensor(hw[:, par, 0:width].rearrange("p (e h) -> p e h", e=experts),
                                   av[:, 0:width].rearrange("p (e h) -> p e h", e=experts),
                                   weights.unsqueeze(2).to_broadcast([P, experts, width // experts]), ALU.mult)\
                    .then_inc(hw_ok, 1)

            def weigh0(q, c, par):
                experts = WD0[c] // H0
                weigh(q, c % 2, g[:, par, c * CE0:c * CE0 + experts], experts, WD0[c])

            def weigh1(q, c, par):
                weigh(q, (CH1 * par + c) % 2, g1[:, par, :], ES1, WD1[c])

            def low_up1(m):
                pool.wait_ge(s1_hi, m + 1)
                at = bass.ds(m * PCU1, PCU1)
                pool.tensor_tensor(w1u_lo[:, at], w1_raw[:, at], w1u_hi[:, at].bitcast(F32),
                                   ALU.subtract).then_inc(s1_lo, 1)

            def with_values(b):
                pool.wait_ge(ct_in, 16)
                pool.wait_ge(ek_ok, EK * b + EK)
                pool.tensor_tensor(ev[:], ek[:], ctx_of(b), ALU.mult).then_inc(ev_ok, 1)
                pool.tensor_tensor(own_v[:], own_k[:], ctx_of(b), ALU.mult).then_inc(ev_ok, 1)

            def divided(b):
                pool.wait_ge(kT_ps, b + 1)
                pool.sem_inc(passed_pool, 1)
                pool.tensor_copy(yt[:, :, 0:1], ctx_of(b)[:, :, 0:1]).then_inc(y_ok, 1)
                pool.wait_ge(wk, WK * b + WK)
                pool.tensor_tensor(yt[:, :, 1:R], own_v[:, :, 1:R], ek[:, :, 1:R], ALU.mult).then_inc(y_ok, 1)

            def low_down1(k):
                pool.wait_ge(s1_hi, NU1 + k + 1)
                at = down1_at(k)
                pool.tensor_tensor(w0_lo[:, at:at + C], w0_raw[:, at:at + C], w0_hi[:, at:at + C].bitcast(F32),
                                   ALU.subtract).then_inc(s1_lo, 1)

            def step0(b, par, first, last):
                q = CH0 * b + LAG
                for k in range(CH0):
                    c, tile_par = (k + LAG) % CH0, par if k < CH0 - LAG else 1 - par
                    if k == 0:
                        if not first:
                            rstd2(b - 1)
                        rstd(b + 1)
                    if k == 1:
                        xT_low(b + 1, 1 - par)
                    if k in (1, 2) and first:
                        low0(NP0 - 3 + k)
                    if k == CH0 - LAG:
                        pool.wait_ge(g_ok, b + 2)
                    if k == 4 and not first:
                        divided(b - 1)
                    (weigh1 if last and c < LAG else weigh0)(q + k, c, tile_par)
                    if k == 2 and not first:
                        with_values(b - 1)
                    if last:
                        for m in DOWNS0[k]:
                            low_down1(m)
                    elif first and k > 1:
                        for m in (2 * k - 4, 2 * k - 3):
                            low_up1(m)
                    elif not first and k in PIECES0:
                        low_up1(GR1 * b + (GR1 + PIECES0.index(k)))

            rstd(0)
            low0(NP0 - NPL)
            xT_low(0, 0)
            low0(NP0 - NPL + 1)
            low0(NP0 - NPL + 2)
            pool.wait_ge(g_ok, 1)
            for c in range(LAG):
                weigh0(c, c, 0)
                if c < LAG - 1:
                    low0(NP0 - NPL + LAG + c)
            step0(0, 0, True, False)
            with pool.Fori(0, (B - 2) // 2) as i:
                for k in range(2):
                    step0(2 * i + (k + 1), 1 - k, False, False)
            step0(B - 1, 1, False, True)

            def step1(b, par, first, last):
                q = CH1 * b + (Q1 + LAG)
                for k in range(CH1 if not last else CH1 - LAG):
                    if k == 0:
                        if first:
                            rstd2(B - 1)
                        if not last:
                            rstd(b + (B + 1))
                    if k == 1 and not last:
                        xT_low(b + (B + 1), 1 - par)
                    if k == CH1 - LAG:
                        pool.wait_ge(g_ok, b + (B + 2))
                    if k == 4 and first:
                        divided(B - 1)
                    weigh1(q + k, (k + LAG) % CH1, par if k < CH1 - LAG else 1 - par)
                    if first:
                        for m in DOWNS1[k]:
                            low_down1(m)
                    if k == 1 and first:
                        with_values(B - 1)

            step1(0, 0, True, False)
            with pool.Fori(0, (B - 2) // 2) as i:
                for k in range(2):
                    step1(2 * i + (k + 1), 1 - k, False, False)
            step1(B - 1, 1, False, True)

        @block.scalar
        def _(act):
            act.wait_ge(small_in, 16)
            act.activation(gt[:], gates_sb, ACT.Tanh).then_inc(setup_act, 1)
            act.wait_ge(setup_dve, 4)
            act.activation(etd[:], tdc[:], ACT.Exp).then_inc(setup_act, 1)
            act.wait_ge(setup_act, 2)
            act.activation(dc[:], etd[:], ACT.Exp, scale=-1.0).then_inc(setup_act, 1)
            for b in range(B):
                act.wait_ge(qT_ps, b + 1)
                act.activation(qt[:, :, b, :], M[b % 4][:, 0:C].rearrange("p (t r) -> p t r", t=NT),
                               ACT.Copy).then_inc(qT_ok, 1)
            for i in range(L0):
                act.wait_ge(w0_in[i], 16)
                for m in range(i * NP0 // L0, (i + 1) * NP0 // L0):
                    at = slice(m * PC0, (m + 1) * PC0)
                    act.activation(w0_hi[:, at], w0_raw[:, at], ACT.Copy).then_inc(s0_hi, 1)

            def turned(n, par):
                act.wait_ge(xT_ps, n + 1)
                act.activation(xT[:].rearrange("p t r -> p (t r)"), TURN, ACT.Copy).then_inc(xT_ok, 1)
                act.activation(xT_hi[:, par].rearrange("p t r -> p (t r)"), TURN, ACT.Copy).then_inc(xT_hi_ok, 1)

            def exp0(b):
                act.wait_ge(lg_ps, b + 1)
                act.activation(es0[:], LG, ACT.Exp, scale=-1.0).then_inc(exp_ok, 1)

            def exp1(b):
                act.wait_ge(nmx_ok, b + 1)
                act.activation(es0[:, 0:E1], LG1, ACT.Exp, bias=nmx[:, 0:1]).then_inc(exp_ok, 1)

            def ek_of(b):
                act.wait_ge(kT_ps, b + 1)
                act.wait_ge(setup_dve, 4)
                for dst, bias in ((ek, nmax), (own_k, umin)):
                    for t in range(NT):
                        act.activation(dst[:, t, :], TURN[:, t * R:(t + 1) * R], ACT.Exp, bias=bias[:, t:t + 1])\
                            .then_inc(ek_ok, 1)

            def silu(q, par, width):
                act.wait_ge(up_ps, q + 1)
                if not (isinstance(q, int) and q == 0):
                    act.wait_ge(av_ok, q)
                act.activation(sil[:, 0:width], U[par][:, 0, 0:width], ACT.Silu).then_inc(sil_ok, 1)

            def high(q, par, width):
                act.wait_ge(hT_ps, q + 1)
                if not (isinstance(q, int) and q < 2):
                    act.wait_ge(down_ps, q - 1)
                n = tiles(width) * P
                act.activation(hT_hi[:, par, 0:n], HT[par][:, 0:n], ACT.Copy).then_inc(hT_hi_ok, 1)

            def split_up1(m):
                at = bass.ds(m * PCU1, PCU1)
                act.activation(w1u_hi[:, at], w1_raw[:, at], ACT.Copy).then_inc(s1_hi, 1)

            def split_down1(k):
                if k % KT == 0:
                    act.wait_ge(down1_in[k // KT], 16)
                at = down1_at(k)
                act.activation(w0_hi[:, at:at + C], w0_raw[:, at:at + C], ACT.Copy).then_inc(s1_hi, 1)

            def step0(b, par, first, last):
                q = CH0 * b + LAG
                for k in range(CH0):
                    silu(q + k, (k + LAG) % 2, width0(k + LAG, last))
                    if k == 1:
                        turned(b + 1, 1 - par)
                    high(q + (k - 2), (k + LAG) % 2, width0(k + 1, last))
                    if last:
                        for m in DOWNS0[k]:
                            split_down1(m)
                    elif first and k > 1:
                        if k == 2:
                            act.wait_ge(w1_in[0], 16)
                        for m in (2 * k - 4, 2 * k - 3):
                            split_up1(m)
                    elif not first and k in SPLITS0:
                        split_up1(GR1 * b + (GR1 + SPLITS0.index(k)))
                    if k == 1:
                        if last:
                            exp1(0)
                        else:
                            exp0(b + 1)
                        if not first:
                            ek_of(b - 1)

            turned(0, 0)
            exp0(0)
            for c in range(LAG):
                silu(c, c % 2, WD0[c])
            high(0, 0, WD0[0])
            step0(0, 0, True, False)
            for i in range(1, L0):
                act.wait_ge(w1_in[i], 16)
            with act.Fori(0, (B - 2) // 2) as i:
                for k in range(2):
                    step0(2 * i + (k + 1), 1 - k, False, False)
            step0(B - 1, 1, False, True)

            def step1(b, par, first, last):
                q = CH1 * b + (Q1 + LAG)
                for k in range(CH1 if not last else CH1 - LAG):
                    upar = (CH1 * par + LAG + k) % 2
                    silu(q + k, upar, width1(k + LAG))
                    if k == 1 and not last:
                        turned(b + (B + 1), 1 - par)
                    high(q + (k - 2), upar, width1(k + 1))
                    if first:
                        for m in DOWNS1[k]:
                            split_down1(m)
                    if k == 1:
                        if not last:
                            exp1(b + 1)
                        if first:
                            ek_of(B - 1)
                if last:
                    high(Q_END - 2, (Q_END - 2) % 2, WD1[CH1 - 2])
                    high(Q_END - 1, (Q_END - 1) % 2, WD1[CH1 - 1])

            step1(0, 0, True, False)
            with act.Fori(0, (B - 2) // 2) as i:
                for k in range(2):
                    step1(2 * i + (k + 1), 1 - k, False, False)
            step1(B - 1, 1, False, True)

        @block.tensor
        def _(pe):
            def turn(dst, src):
                return pe.transpose(dst, src, ident[:])

            pe.wait_ge(const_ok, 4)

            def q_turn(b):
                pe.wait_ge(qn_ok, b + 1)
                if b >= 4:
                    pe.wait_ge(qT_ok, b - 3)
                for t in range(NT):
                    mm = turn(M[b % 4][:, t * P:(t + 1) * P], qn[:, b, t * P:(t + 1) * P])
                mm.then_inc(qT_ps, 1)

            def conv(hg, h, t):
                k = NT * h + t
                tap, bank = tz[:, hg % 2, h], Y[k % Y0]
                if t == 0:
                    if h == 0:
                        if hg == 0:
                            pe.wait_ge(toep0_in, 16)
                        else:
                            pe.wait_ge(toep_in, 16 * hg)
                    if hg > 0 and h in Z0_POOL:
                        pe.wait_ge(z0_pool, len(Z0_POOL) * (hg - 1) + Z0_POOL.index(h) + 1)
                    else:
                        pe.wait_ge(z_dve, z_dve_count(hg, h))
                pe.wait_ge(prod_ok, BLK * hg + k + 1)
                if t == 0:
                    mm = pe.matmul(bank, tap[:, 0:P], z[:, 0, h, :], start=True, stop=True)
                else:
                    pe.matmul(bank, tap[:, P:2 * P], z[:, 0, h, :], start=True, stop=False)
                    pe.wait_ge(z_pool, HG * hg + h + 1)
                    mm = pe.matmul(bank, tap[:, 0:P], z[:, 1, h, :], start=False, stop=True)
                mm.then_inc(conv_ps, 1)

            conv(0, 0, 0)
            for b in range(B):
                q_turn(b)
            conv(0, 0, 1)
            for hg in range(NHG):
                for h in range(1 if hg == 0 else 0, HG):
                    for t in range(NT):
                        conv(hg, h, t)

            pe.wait_ge(oc_ok, BLK * NHG)
            for b in range(B):
                for t in range(NT):
                    mm = turn(M[b][:, t * P:(t + 1) * P], oc[:, t, b, :])
                mm.then_inc(oT_ps, 1)

            def pre(n):
                pe.wait_ge(xn_ok, n + 1)
                for t in range(NT):
                    mm = turn(TURN[:, t * P:(t + 1) * P], xn[:, t * P:(t + 1) * P])
                mm.then_inc(xT_ps, 1)

            def logits(n, w, dst):
                pe.wait_ge(xT_hi_ok, n + 1)
                if not (isinstance(n, int) and n == 0):
                    pe.wait_ge(exp_ok, n)
                for t in range(NT):
                    mm = pe.matmul(dst, xT[:, t, :], w[:, t, :], start=(t == 0), stop=(t == NT - 1))
                mm.then_inc(lg_ps, 1)

            def places(b):
                pe.wait_ge(mask_ok, b + 1)
                pe.wait_ge(run_ok, b + 1)
                pe.matmul(PS, tri[:], maskb[:], start=True, stop=False)
                pe.matmul(PS, ones[:], run[:], start=False, stop=True).then_inc(pos_ps, 1)

            def up(q, n, xpar, c, upar, w, widths):
                width = widths[c]
                if not (isinstance(q, int) and q < 2):
                    pe.wait_ge(av_ok, q - 1)
                if isinstance(q, int) and q < 2:
                    pe.wait_ge(x1_ok, B - 2 + 2 * q)
                if isinstance(q, int) and q < CH0:
                    pe.wait_ge(s0_lo, pieces0((NT - 1) * UW0 + 2 * (c * CP + width)))
                if c == 0:
                    pe.wait_ge(xT_hi_ok, n + 1)
                parts = [(xT_hi, t, low) for t in range(NT) for low in (0, 1)] + [(xT_lo, t, 0) for t in range(NT)]
                for i, (xp, t, low) in enumerate(parts):
                    if c == 0 and i == 2 * NT:
                        pe.wait_ge(xT_lo_ok, n + 1)
                    for half in range(2):
                        a = 2 * c * widths[0] + half * width
                        mm = pe.matmul(U[upar][:, half, 0:width], xp[:, xpar, t, :], w(low, t, a, a + width),
                                       start=(i == 0), stop=(i == len(parts) - 1))
                mm.then_inc(up_ps, 1)

            def turn_h(q, par, width):
                pe.wait_ge(hw_ok, q + 1)
                if not (isinstance(q, int) and q < 2):
                    pe.wait_ge(hT_lo_ok, q - 1)
                for k in range(tiles(width)):
                    mm = turn(HT[par][:, k * P:(k + 1) * P], hw[:, par, k * P:(k + 1) * P])
                mm.then_inc(hT_ps, 1)

            def down(q, par, c, widths, w, free=None):
                n, chunks = tiles(widths[c]), len(widths)
                if isinstance(q, int) and q < CH0:
                    pe.wait_ge(s0_lo, pieces0(NT * UW0 + (c * KT + n) * C))
                pe.wait_ge(hT_hi_ok, q + 1)
                if free:
                    pe.wait_ge(*free)
                parts = [(hT_hi, k, low) for k in range(n) for low in (0, 1)] + [(hT_lo, k, 0) for k in range(n)]
                for i, (h, k, low) in enumerate(parts):
                    if i == 2 * n:
                        pe.wait_ge(hT_lo_ok, q + 1)
                    mm = pe.matmul(DN[:, 0:C], h[:, par, k * P:(k + 1) * P], w(low, c * KT + k),
                                   start=(c == 0 and i == 0), stop=(c == chunks - 1 and i == len(parts) - 1))
                mm.then_inc(down_ps, 1)

            def kT(b):
                pe.wait_ge(xn2_ok, b + 1)
                pe.wait_ge(xT_hi_ok, b + 3)
                for t in range(NT):
                    mm = turn(TURN[:, t * P:(t + 1) * P], xn2[:, t * P:(t + 1) * P])
                mm.then_inc(kT_ps, 1)

            def yT(b):
                pe.wait_ge(y_ok, 2 * b + 2)
                for t in range(NT):
                    mm = turn(TURN[:, t * P:(t + 1) * P], yt[:, t, :])
                mm.then_inc(yT_ps, 1)

            def step0(b, par, first, last):
                q = CH0 * b + LAG
                for k in range(CH0):
                    c = (k + LAG) % CH0
                    if k < CH0 - LAG:
                        up(q + k, b, par, c, c % 2, up0, WD0)
                    elif last:
                        if c == 0:
                            pe.wait_ge(s1_lo, NU1)
                        up(q + k, b + 1, 1 - par, c, c % 2, up1, WD1)
                    else:
                        up(q + k, b + 1, 1 - par, c, c % 2, up0, WD0)
                    turn_h(q + (k - 2), c % 2, width0(k + 1, last))
                    if k == 1:
                        pre(b + 1)
                    down(q + (k - LAG), (c + 1) % 2, k, WD0, down0, (x2_ok, b) if k == 0 and not first else None)
                    if k == 1:
                        if not first:
                            kT(b - 1)
                        logits(b + 1, wg1 if last else wg0, LG1 if last else LG)
                    if k == CH0 - LAG and not last:
                        places(b + 1)
                if not first:
                    yT(b - 1)

            pre(0)
            logits(0, wg0, LG)
            for c in range(LAG):
                up(c, 0, 0, c, c % 2, up0, WD0)
                if c == 1:
                    places(0)
            turn_h(0, 0, WD0[0])
            step0(0, 0, True, False)
            with pe.Fori(0, (B - 2) // 2) as i:
                for k in range(2):
                    step0(2 * i + (k + 1), 1 - k, False, False)
            step0(B - 1, 1, False, True)

            def step1(b, par, first, last):
                q = CH1 * b + (Q1 + LAG)
                for k in range(CH1 if not last else CH1 - LAG):
                    c, own = (k + LAG) % CH1, k < CH1 - LAG
                    upar = (CH1 * par + LAG + k) % 2
                    up(q + k, b + (B if own else B + 1), par if own else 1 - par, c, upar, up1, WD1)
                    turn_h(q + (k - 2), upar, width1(k + 1))
                    if k == 1 and not last:
                        pre(b + (B + 1))
                    if first:
                        pe.wait_ge(s1_lo, NU1 + KT * k + tiles(WD1[k]))
                    down(q + (k - LAG), 1 - upar, k, WD1, down1,
                         None if k else (x2_ok, B) if first else (x4_ok, b))
                    if k == 1:
                        if first:
                            kT(B - 1)
                        if not last:
                            logits(b + (B + 1), wg1, LG1)
                if first:
                    yT(B - 1)

            step1(0, 0, True, False)
            with pe.Fori(0, (B - 2) // 2) as i:
                for k in range(2):
                    step1(2 * i + (k + 1), 1 - k, False, False)
            step1(B - 1, 1, False, True)
            for c in range(CH1 - LAG, CH1):
                q = Q_END - CH1 + c
                if c < CH1 - 1:
                    turn_h(q + 1, (q + 1) % 2, WD1[c + 1])
                down(q, q % 2, c, WD1, down1)

        @block.vector
        def _(dve):
            def after(ins, s, value):
                ins.then_inc(s, 1)
                dve.wait_ge(s, value)
                dve.sem_inc(passed_dve, 1)

            dve.wait_ge(pad_in, 16)
            dve.tensor_tensor(padded[:, P - 1:P], padded[:, P - 1:P], padded[:, 3 * P:3 * P + 1], ALU.add)\
                .then_inc(with_d, 1)
            dve.wait_ge(iota_ok, 1)
            dve.tensor_copy(iota0[:], iota_i[:]).then_inc(setup_dve, 1)
            dve.sem_inc(prod_ok, Y0)

            def z_of(hg, h):
                rows = cr[:, 0, :, bass.ds(hg * (HG * HD) + h * HD, HD)]
                dve.tensor_tensor(z[:, 0, h, :].rearrange("p (b i j) -> p b i j", b=B, i=HD),
                                  rows.unsqueeze(3).to_broadcast([P, B, HD, HD]),
                                  rows.unsqueeze(2).to_broadcast([P, B, HD, HD]), ALU.mult).then_inc(z_dve, 1)

            dve.wait_ge(ctx_in[0], 16)
            for h in range(HG):
                z_of(0, h)

            for i in range(2):
                half = range(i * HB, (i + 1) * HB)
                dve.wait_ge(x_in[i], 16)
                for b in half:
                    dve.bn_stats(bstq[:, b, :], xs[:, b, :]).then_inc(qstep, 1)
                dve.wait_ge(qstep, (2 * i + 1) * HB)
                dve.sem_inc(passed_dve, 1)
                for b in half:
                    dve.bn_aggr(mvq[:, b, :], bstq[:, b, :]).then_inc(qstep, 1)
                dve.wait_ge(qstep, (2 * i + 2) * HB)
                dve.tensor_scalar(veq[:, i * HB:(i + 1) * HB], mvq[:, i * HB:(i + 1) * HB, 1], LN_EPS, None,
                                  ALU.add).then_inc(qvar_ok, 1)
            for b in range(B):
                if b % HB == 0:
                    dve.wait_ge(qrstd_ok, b // HB + 1)
                dve.tensor_scalar(qn[:, b, :], xs[:, b, :], mvq[:, b, 0:1], rsq[:, b:b + 1],
                                  ALU.subtract, ALU.mult).then_inc(qn_ok, 1)
            dve.wait_ge(small_in, 16)
            dve.tensor_scalar(nmax[:], fs, 0.0, -1.0, ALU.max, ALU.mult).then_inc(setup_dve, 1)
            dve.tensor_scalar(umin[:], fs, 0.0, None, ALU.min).then_inc(setup_dve, 1)
            dve.tensor_scalar(tdc[:], td, 80.0, None, ALU.min).then_inc(setup_dve, 1)
            dve.wait_ge(qT_ok, B)

            def sum_rows(hg, k):
                h, t = k // NT, k % NT
                dve.wait_ge(prod_ok, BLK * hg + (k + 1 + Y0))
                dve.tensor_reduce(oc[:, t, :, bass.ds(hg * (HG * HD) + h * HD, HD)],
                                  prod[:, k % 4, :].rearrange("p (b i j) -> p b j i", b=B, i=HD),
                                  AX.X, ALU.add).then_inc(oc_ok, 1)

            def step(hg, last):
                for k in range(BLK):
                    h, t = k // NT, k % NT
                    dve.wait_ge(conv_ps, BLK * hg + (k + 1))
                    if k >= 4:
                        dve.wait_ge(oc_ok, BLK * hg + (k - 3))
                    q = qt[:, t, :, bass.ds(hg * (HG * HD) + h * HD, HD)]
                    dve.tensor_tensor(prod[:, k % 4, :].rearrange("p (b i j) -> p b i j", b=B, i=HD),
                                      Y[k % Y0].rearrange("p (b i j) -> p b i j", b=B, i=HD),
                                      q.unsqueeze(3).to_broadcast([P, B, HD, HD]), ALU.mult)\
                        .then_inc(prod_ok, 1)
                    if t == NT - 1 and not last and h not in Z0_POOL:
                        z_of(hg + 1, h)
                    if k > 0:
                        sum_rows(hg, k - 1)
                sum_rows(hg, BLK - 1)
                dve.wait_ge(oc_ok, BLK * (hg + 1))

            with dve.Fori(0, NHG - 1) as hg:
                step(hg, False)
            step(NHG - 1, True)

            def tile_of(b):
                return dyn(xs, b)

            def stats(n, b, ready, count):
                dve.wait_ge(ready, count)
                dve.sem_inc(passed_dve, 1)
                after(dve.bn_stats(bst[:], tile_of(b)), ln_step, 2 * n + 1)
                after(dve.bn_aggr(mv[:], bst[:]), ln_step, 2 * n + 2)
                dve.tensor_scalar(ve[:], mv[:, 1:2], LN_EPS, None, ALU.add).then_inc(var_ok, 1)

            def normed(n, b):
                if not (isinstance(n, int) and n == 0):
                    dve.wait_ge(xT_ps, n)
                dve.wait_ge(rstd_ok, n + 1)
                dve.tensor_scalar(xn[:], tile_of(b), mv[:, 0:1], rs[:, 0:1], ALU.subtract, ALU.mult)\
                    .then_inc(xn_ok, 1)

            def add_conv(b):
                dve.wait_ge(oT_ps, b + 1)
                dve.scalar_tensor_tensor(out=xs[:, b, :], in0=M[b][:, 0:C], scalar=gt[:, 0:1],
                                         in1=xs[:, b, :], op0=ALU.mult, op1=ALU.add).then_inc(x1_ok, 1)

            dve.wait_ge(setup_act, 3)
            add_conv(0)
            stats(0, 0, x1_ok, 1)
            add_conv(1)
            add_conv(2)
            normed(0, 0)
            for b in range(3, B):
                add_conv(b)
            dve.memset(run[:], 0.0).then_inc(run_ok, 1)
            dve.memset(sa[:, :, 0:1], 0.0).then_inc(pad_ok, 1)
            dve.memset(sb_[:, :, 0:1], 1.0).then_inc(pad_ok, 1)
            dve.memset(g[:, :, E0:ES0], 1.0).then_inc(pad_ok, 1)
            dve.wait_ge(pad_ok, 3)

            def best(top, experts, at):
                after(dve.max(v8[:], sc[:, 0:experts]), route, at + 1)
                after(dve.max_index(i8[:], v8[:], sc[:, 0:experts]), route, at + 2)
                after(dve.tensor_copy(f8[:], i8[:]), route, at + 3)
                dve.tensor_tensor(eq[:, 0:top, 0:experts],
                                  iota0[:, 0:experts].unsqueeze(1).to_broadcast([P, top, experts]),
                                  f8[:, 0:top].unsqueeze(2).to_broadcast([P, top, experts]),
                                  ALU.is_equal).then_inc(route, 1)

            def chosen(top, experts, at):
                dve.wait_ge(route, at + 4)
                after(dve.tensor_reduce(mask[:, 0:experts], eq[:, 0:top, 0:experts].rearrange("p k e -> p e k"),
                                        AX.X, ALU.add), route, at + 5)

            def route0(b):
                at = RT0 * b
                dve.wait_ge(exp_ok, b + 1)
                after(dve.tensor_scalar(sc[:], es0[:], 1.0, None, ALU.add), route, at + 1)
                after(dve.reciprocal(sc[:], sc[:]), route, at + 2)
                best(TOP0, E0, at + 2)

            def chosen0(b):
                chosen(TOP0, E0, RT0 * b + 2)
                dve.tensor_copy(maskb[:], mask[:]).then_inc(mask_ok, 1)

            def scores0(b):
                at = RT0 * b + 7
                dve.tensor_tensor(msc[:], mask[:], sc[:], ALU.mult).then_inc(route, 1)
                dve.tensor_reduce(den[:], v8[:, 0:TOP0], AX.X, ALU.add).then_inc(route, 1)
                dve.wait_ge(route, at + 2)
                dve.reciprocal(rden[:], den[:]).then_inc(route, 1)

            def weights0(b, par):
                at = RT0 * b + 10
                dve.wait_ge(pos_ps, b + 1)
                if not (isinstance(b, int) and b == 0):
                    dve.wait_ge(hw_ok, CH0 * b - CH0 + 1)
                dve.wait_ge(route, at)
                after(dve.scalar_tensor_tensor(out=g[:, par, 0:E0], in0=PS, scalar=float(CAP0), in1=msc[:],
                                               op0=ALU.is_lt, op1=ALU.mult), route, at + 1)
                dve.tensor_scalar(g[:, par, 0:E0], g[:, par, 0:E0], rden[:, 0:1], None, ALU.mult).then_inc(g_ok, 1)
                dve.tensor_tensor(run[:], run[:], maskb[:], ALU.add).then_inc(run_ok, 1)

            def logit_max(b):
                dve.wait_ge(lg_ps, b + (B + 1))
                dve.tensor_reduce(nmx[:], LG1, AX.X, ALU.max, negate=True).then_inc(nmx_ok, 1)

            def route1(b):
                at = RT1 * b + RT0 * B
                dve.wait_ge(exp_ok, b + (B + 1))
                after(dve.tensor_reduce(den[:], es0[:, 0:E1], AX.X, ALU.add), route, at + 1)
                after(dve.reciprocal(rden[:], den[:]), route, at + 2)
                after(dve.tensor_scalar(sc[:, 0:E1], es0[:, 0:E1], rden[:, 0:1], None, ALU.mult), route, at + 3)
                best(TOP1, E1, at + 3)

            def weights1(b, par):
                at = RT1 * b + RT0 * B
                chosen(TOP1, E1, at + 3)
                dve.tensor_tensor(msc[:, 0:E1], mask[:, 0:E1], sc[:, 0:E1], ALU.mult).then_inc(route, 1)
                dve.tensor_reduce(den[:], v8[:, 0:TOP1], AX.X, ALU.add).then_inc(route, 1)
                dve.wait_ge(route, at + 10)
                after(dve.reciprocal(rden[:], den[:]), route, at + 11)
                dve.tensor_scalar(g1[:, par, 0:E1], msc[:, 0:E1], rden[:, 0:1], None, ALU.mult).then_inc(g_ok, 1)

            def act_of(q, par, width):
                dve.wait_ge(sil_ok, q + 1)
                if not (isinstance(q, int) and q == 0):
                    dve.wait_ge(hw_ok, q)
                dve.tensor_tensor(av[:, 0:width], sil[:, 0:width], U[par][:, 1, 0:width], ALU.mult).then_inc(av_ok, 1)

            def low(q, par, width):
                dve.wait_ge(hT_hi_ok, q + 1)
                n = tiles(width) * P
                dve.tensor_tensor(hT_lo[:, par, 0:n], HT[par][:, 0:n], hT_hi[:, par, 0:n].bitcast(F32),
                                  ALU.subtract).then_inc(hT_lo_ok, 1)

            def add(q, b, gate, done):
                dve.wait_ge(down_ps, q)
                dve.scalar_tensor_tensor(out=tile_of(b), in0=DN[:, 0:C], scalar=gt[:, gate:gate + 1],
                                         in1=tile_of(b), op0=ALU.mult, op1=ALU.add).then_inc(done, 1)

            def stats2(b):
                dve.wait_ge(x2_ok, b + 1)
                dve.sem_inc(passed_dve, 1)
                after(dve.bn_stats(bst2[:], tile_of(b)), ln2_step, 2 * b + 1)

            def variance2(b):
                after(dve.bn_aggr(mv2[:], bst2[:]), ln2_step, 2 * b + 2)
                dve.tensor_scalar(ve2[:], mv2[:, 1:2], LN_EPS, None, ALU.add).then_inc(var2_ok, 1)

            def normed2(b):
                dve.wait_ge(rstd2_ok, b + 1)
                dve.tensor_scalar(xn2[:], tile_of(b), mv2[:, 0:1], rs2[:, 0:1], ALU.subtract, ALU.mult)\
                    .then_inc(xn2_ok, 1)

            def scan(b, dst, src, ready):
                dve.wait_ge(*ready)
                for t in range(NT):
                    dve.tensor_tensor_scan(dst[:, t, 1:R + 1], dc[:, t:t + 1].to_broadcast([P, R]),
                                           src[:, t, :], 0.0, ALU.mult, ALU.add).then_inc(wk, 1)

            def denominator(b):
                dve.wait_ge(wk, WK * b + 2)
                dve.wait_ge(ev_ok, EV * b + 1)
                dve.tensor_tensor(ek[:], own_k[:], sb_[:, :, 0:R], ALU.add).then_inc(wk, 1)

            def numerator(b):
                dve.wait_ge(wk, WK * b + 6)
                dve.wait_ge(ev_ok, EV * b + EV)
                dve.tensor_tensor(own_v[:], own_v[:], sa[:, :, 0:R], ALU.add).then_inc(wk, 1)

            def inverse(b, t):
                dve.wait_ge(wk, WK * b + 3)
                dve.reciprocal(ek[:, t, :], ek[:, t, :]).then_inc(wk, 1)

            def add_y(b):
                dve.wait_ge(yT_ps, b + 1)
                dve.scalar_tensor_tensor(out=tile_of(b), in0=TURN, scalar=gt[:, 1:2],
                                         in1=tile_of(b), op0=ALU.mult, op1=ALU.add).then_inc(x3_ok, 1)

            def step0(b, par, first, last):
                q = CH0 * b + LAG

                def act(k):
                    act_of(q + k, (k + LAG) % 2, width0(k + LAG, last))

                def low_of(k):
                    low(q + (k - 2), (k + LAG) % 2, width0(k + 1, last))

                if not first:
                    stats2(b - 1)
                    variance2(b - 1)
                if last:
                    stats(B, 0, x3_ok, 1)
                else:
                    stats(b + 1, b + 1, x1_ok, B)
                act(0)
                if not first:
                    normed2(b - 1)
                normed(b + 1, 0 if last else b + 1)
                low_of(0)
                act(1)
                low_of(1)
                if last:
                    logit_max(0)
                    route1(0)
                else:
                    route0(b + 1)
                act(2)
                low_of(2)
                if last:
                    weights1(0, 1 - par)
                else:
                    chosen0(b + 1)
                if not first:
                    scan(b - 1, sb_, ek, (ek_ok, b * EK))
                    denominator(b - 1)
                act(3)
                low_of(3)
                if not last:
                    scores0(b + 1)
                if not first:
                    inverse(b - 1, 0)
                    scan(b - 1, sa, ev, (ev_ok, EV * b - 1))
                if not last:
                    weights0(b + 1, 1 - par)
                if not first:
                    numerator(b - 1)
                    inverse(b - 1, 1)
                act(4)
                low_of(4)
                act(5)
                low_of(5)
                add(q + LAG, b, 2, x2_ok)
                if not first:
                    add_y(b - 1)

            route0(0)
            act_of(0, 0, WD0[0])
            chosen0(0)
            scores0(0)
            weights0(0, 0)
            for c in range(1, LAG):
                act_of(c, c % 2, WD0[c])
            low(0, 0, WD0[0])
            step0(0, 0, True, False)
            with dve.Fori(0, (B - 2) // 2) as i:
                for k in range(2):
                    step0(2 * i + (k + 1), 1 - k, False, False)
            step0(B - 1, 1, False, True)

            def step1(b, par, first, last):
                q = CH1 * b + (Q1 + LAG)
                last_b = B - 1

                def act(k):
                    act_of(q + k, (CH1 * par + LAG + k) % 2, width1(k + LAG))

                def low_of(k):
                    low(q + (k - 2), (CH1 * par + LAG + k) % 2, width1(k + 1))

                if first:
                    stats2(last_b)
                    variance2(last_b)
                if not last:
                    stats(b + (B + 1), b + 1, x3_ok, b + 2)
                act(0)
                if first:
                    normed2(last_b)
                if not last:
                    normed(b + (B + 1), b + 1)
                low_of(0)
                act(1)
                low_of(1)
                if last:
                    low_of(2)
                    low_of(3)
                    add(Q_END, b, 3, x4_ok)
                    return
                logit_max(b + 1)
                if first:
                    scan(last_b, sb_, ek, (ek_ok, B * EK))
                route1(b + 1)
                act(2)
                low_of(2)
                weights1(b + 1, 1 - par)
                if first:
                    denominator(last_b)
                if first:
                    inverse(last_b, 0)
                    scan(last_b, sa, ev, (ev_ok, B * EV - 1))
                    numerator(last_b)
                act(3)
                low_of(3)
                if first:
                    inverse(last_b, 1)
                act(4)
                low_of(4)
                add(q + 2, b, 3, x4_ok)
                if first:
                    add_y(last_b)

            step1(0, 0, True, False)
            with dve.Fori(0, (B - 2) // 2) as i:
                for k in range(2):
                    step1(2 * i + (k + 1), 1 - k, False, False)
            step1(B - 1, 1, False, True)


_SHAPE = (B, R, C)


def kernel(x, ctx_2048, g_xattn, g_ffn, L0_xattn_ssm_kernel, L0_xattn_D, L0_ffn_w_gate, L0_ffn_w_shared_up,
           L0_ffn_w_shared_down, L0_ffn_w_up, L0_ffn_w_down, L1_xattn_time_decay, L1_xattn_time_first,
           L1_ffn_gate_weight, L1_ffn_w_gate, L1_ffn_w_up, L1_ffn_w_down, L1_ffn_w_shared_gate,
           L1_ffn_w_shared_up, L1_ffn_w_shared_down):
    import numpy as np
    import concourse.bacc as bacc
    from concourse.bass_utils import run_bass_kernel_spmd as run

    f32 = np.float32

    def channels_first(a):
        return a.reshape(NT, P, -1).transpose(1, 0, 2).reshape(P, -1)

    def rows_first(a):
        return a.reshape(-1, P, C).transpose(1, 0, 2).reshape(P, -1)

    x = np.asarray(x)
    ctx = np.asarray(ctx_2048).transpose(2, 0, 1).reshape(NT, P, B, R)
    ctx_t = ctx.transpose(1, 0, 2, 3)
    ctx_rev = ctx[:, ::-1].transpose(1, 0, 2, 3)
    taps = np.asarray(L0_xattn_ssm_kernel)
    conv_pad = np.concatenate([np.zeros((HEADS, P - 1), f32), taps, np.zeros((HEADS, 1), f32),
                               np.asarray(L0_xattn_D).reshape(HEADS, 1)], axis=1)

    def gate_value(gate, value, widths):
        ends = np.cumsum(widths)
        return channels_first(np.concatenate([w[:, e - n:e] for e, n in zip(ends, widths) for w in (gate, value)],
                                             axis=1))

    def padded_rows(w):
        return rows_first(np.concatenate([w, np.zeros((-len(w) % P, C), f32)]))

    up0, sh0 = np.asarray(L0_ffn_w_up), np.asarray(L0_ffn_w_shared_up)
    w0 = np.concatenate([
        gate_value(np.concatenate([up0[:, :, :H0].transpose(1, 0, 2).reshape(C, -1), sh0[:, HS0:]], axis=1),
                   np.concatenate([up0[:, :, H0:].transpose(1, 0, 2).reshape(C, -1), sh0[:, :HS0]], axis=1), WD0),
        padded_rows(np.concatenate([np.asarray(L0_ffn_w_down).reshape(-1, C), np.asarray(L0_ffn_w_shared_down)])),
    ], axis=1)

    def by_chunk(experts, shared):
        w = np.concatenate([experts, shared]).reshape(ES1, H1, C)
        return [w[:, a:a + CF1].reshape(-1, C) for a in range(0, H1, CF1)]

    gate1 = np.concatenate(by_chunk(np.asarray(L1_ffn_w_gate).reshape(-1, C), np.asarray(L1_ffn_w_shared_gate))).T
    value1 = np.concatenate(by_chunk(np.asarray(L1_ffn_w_up).reshape(-1, C), np.asarray(L1_ffn_w_shared_up))).T
    down1 = by_chunk(np.asarray(L1_ffn_w_down).transpose(0, 2, 1).reshape(-1, C), np.asarray(L1_ffn_w_shared_down).T)
    w1 = np.concatenate([gate_value(gate1, value1, WD1)] + [padded_rows(w) for w in down1], axis=1)

    def on_all(a):
        return np.broadcast_to(np.asarray(a).reshape(1, -1), (P, np.size(a)))

    small = np.concatenate([
        on_all(g_xattn), on_all(g_ffn),
        np.asarray(L1_xattn_time_decay).reshape(NT, P).T, np.asarray(L1_xattn_time_first).reshape(NT, P).T,
        channels_first(np.asarray(L0_ffn_w_gate)), channels_first(np.asarray(L1_ffn_gate_weight).T),
    ], axis=1)

    arrays = {"small": small, "x": x, "ctx_t": ctx_t, "ctx_rev": ctx_rev, "conv_pad": conv_pad, "w0": w0, "w1": w1}
    arrays = {f"in_{k}": np.ascontiguousarray(v) for k, v in arrays.items()}
    nc = bacc.Bacc("TRN2", target_bir_lowering=False, num_devices=1)
    args = [nc.dram_tensor(k, v.shape, F32, kind="ExternalInput").ap() for k, v in arrays.items()]
    args.append(nc.dram_tensor("taps_with_d", (HEADS, 3 * P), F32, kind="Internal").ap())
    args.append(nc.dram_tensor("out_x", _SHAPE, F32, kind="ExternalOutput").ap())
    build(nc, *args)
    r = run(nc, [arrays], core_ids=[0])
    return r.results[0]["out_x"]
```
